# Optimizing a Trainium2 kernel written in Bass

```python
import numpy as np
import jax
import jax.numpy as jnp

def _softmax(x, axis=-1):
    return jax.nn.softmax(x, axis=axis)

def _gelu(x):
    return jax.nn.gelu(x, approximate=True)

def _silu(x):
    return jax.nn.silu(x)

def _sigmoid(x):
    return jax.nn.sigmoid(x)

def _layernorm(x, axis=-1, eps=1e-05):
    m = jnp.mean(x, axis=axis, keepdims=True)
    v = jnp.var(x, axis=axis, keepdims=True)
    return (x - m) / jnp.sqrt(v + eps)

def _scatter_add(tgt, idx, src, axis=0):
    return tgt.at[idx].add(src)

def _segment_sum(src, seg, n):
    return jax.ops.segment_sum(src, seg, n)
kernel_name = 'mk_macaron_d1_jaxref_r4_5633aa'

def setup_inputs(seed: int=0):
    np.random.seed(seed)
    _w = jnp.asarray

    def _L0_attn_setup():
        import math
        import jax, jax.numpy as jnp
        import numpy as np
        EMB = 256
        HEADS = 16
        HEAD_DIM = EMB // HEADS

        def _srms_norm(x, eps=1e-12):
            dtype = x.dtype
            xf = x.astype(jnp.float32)
            scale = 1.0 / math.sqrt(x.shape[-1])
            n = jnp.linalg.norm(xf * scale, axis=-1, keepdims=True)
            return (xf / jnp.maximum(n, eps)).astype(dtype)
        key = jax.random.key(seed)
        ks = jax.random.split(key, 6)
        b, l = (4, 1024)
        x = jax.random.normal(ks[0], (b, l, EMB), dtype=jnp.float32)
        std = math.sqrt(2.0 / (EMB + EMB))
        Wq = jax.random.normal(ks[1], (EMB, EMB), dtype=jnp.float32) * std
        Wk = jax.random.normal(ks[2], (EMB, EMB), dtype=jnp.float32) * std
        Wv = jax.random.normal(ks[3], (EMB, EMB), dtype=jnp.float32) * std
        Wu = jax.random.normal(ks[4], (EMB, EMB), dtype=jnp.float32) * std
        Wo = jax.random.normal(ks[5], (EMB, EMB), dtype=jnp.float32) * std
        return {'x': x, 'Wq': Wq, 'Wk': Wk, 'Wv': Wv, 'Wu': Wu, 'Wo': Wo}
    _L0_attn_in = _L0_attn_setup()

    def _L0_ffn_setup():
        import jax, jax.numpy as jnp
        import numpy as np
        DIM = 256

        def _reference_tuple_inner(x, W_r, W_k, W_v, mu_r, mu_k):
            B, T, C = x.shape
            x_prev = jnp.concatenate([jnp.zeros((B, 1, C), x.dtype), x[:, :-1, :]], axis=1)
            xr = mu_r * x + (1.0 - mu_r) * x_prev
            xk = mu_k * x + (1.0 - mu_k) * x_prev
            r = jax.nn.sigmoid(jnp.einsum('btc,dc->btd', xr, W_r))
            k = jnp.einsum('btc,dc->btd', xk, W_k)
            k_act = jnp.square(jax.nn.relu(k))
            out = r * jnp.einsum('btc,dc->btd', k_act, W_v)
            new_state = x[:, -1, :]
            return (out, new_state)
        key = jax.random.key(seed)
        ks = jax.random.split(key, 6)
        B, T, C = (8, 512, DIM)
        x = jax.random.normal(ks[0], (B, T, C), dtype=jnp.float32)
        s = 1.0 / np.sqrt(C)
        W_r = jax.random.uniform(ks[1], (C, C), jnp.float32, -s, s)
        W_k = jax.random.uniform(ks[2], (C, C), jnp.float32, -s, s)
        W_v = jax.random.uniform(ks[3], (C, C), jnp.float32, -s, s)
        mu_r = jax.random.uniform(ks[4], (C,), jnp.float32)
        mu_k = jax.random.uniform(ks[5], (C,), jnp.float32)
        return {'x': x, 'W_r': W_r, 'W_k': W_k, 'W_v': W_v, 'mu_r': mu_r, 'mu_k': mu_k}
    _L0_ffn_in = _L0_ffn_setup()
    _d = {'L0_attn_x': _L0_attn_in['x'], 'L0_attn_Wq': _L0_attn_in['Wq'], 'L0_attn_Wk': _L0_attn_in['Wk'], 'L0_attn_Wv': _L0_attn_in['Wv'], 'L0_attn_Wu': _L0_attn_in['Wu'], 'L0_attn_Wo': _L0_attn_in['Wo'], 'L0_ffn_W_r': _L0_ffn_in['W_r'], 'L0_ffn_W_k': _L0_ffn_in['W_k'], 'L0_ffn_W_v': _L0_ffn_in['W_v'], 'L0_ffn_mu_r': _L0_ffn_in['mu_r'], 'L0_ffn_mu_k': _L0_ffn_in['mu_k']}
    _x0 = _d['L0_attn_x']
    _d['L0_attn_x'] = jax.random.normal(jax.random.fold_in(jax.random.key(seed), 1), (2, 2048, 256), dtype=_x0.dtype)
    del _x0
    return _d

def reference(L0_attn_x, L0_attn_Wq, L0_attn_Wk, L0_attn_Wv, L0_attn_Wu, L0_attn_Wo, L0_ffn_W_r, L0_ffn_W_k, L0_ffn_W_v, L0_ffn_mu_r, L0_ffn_mu_k):

    def _L0_attn_ref(x, Wq, Wk, Wv, Wu, Wo):
        import math
        import jax, jax.numpy as jnp
        import numpy as np
        EMB = 256
        HEADS = 16
        HEAD_DIM = EMB // HEADS

        def _srms_norm(x, eps=1e-12):
            dtype = x.dtype
            xf = x.astype(jnp.float32)
            scale = 1.0 / math.sqrt(x.shape[-1])
            n = jnp.linalg.norm(xf * scale, axis=-1, keepdims=True)
            return (xf / jnp.maximum(n, eps)).astype(dtype)
        b, l, d = x.shape
        h, hd = (HEADS, HEAD_DIM)
        scale = math.sqrt(hd)

        def proj(W):
            return jnp.einsum('bld,ed->ble', x, W).reshape(b, l, h, hd).transpose(0, 2, 1, 3)
        q = jax.nn.relu(proj(Wq)) / scale
        k = jax.nn.relu(proj(Wk)) / scale
        v = proj(Wv)
        u = jax.nn.silu(proj(Wu))
        kv = jnp.einsum('bhlk,bhlv->bhkv', k, v)
        out = jnp.einsum('bhlk,bhkv->bhlv', q, kv)
        out = _srms_norm(out) * u
        out = out.transpose(0, 2, 1, 3).reshape(b, l, d)
        return jnp.einsum('bld,ed->ble', out, Wo)

    def _L0_ffn_ref(x, W_r, W_k, W_v, mu_r, mu_k):
        import jax, jax.numpy as jnp
        import numpy as np
        DIM = 256

        def _reference_tuple_inner(x, W_r, W_k, W_v, mu_r, mu_k):
            B, T, C = x.shape
            x_prev = jnp.concatenate([jnp.zeros((B, 1, C), x.dtype), x[:, :-1, :]], axis=1)
            xr = mu_r * x + (1.0 - mu_r) * x_prev
            xk = mu_k * x + (1.0 - mu_k) * x_prev
            r = jax.nn.sigmoid(jnp.einsum('btc,dc->btd', xr, W_r))
            k = jnp.einsum('btc,dc->btd', xk, W_k)
            k_act = jnp.square(jax.nn.relu(k))
            out = r * jnp.einsum('btc,dc->btd', k_act, W_v)
            new_state = x[:, -1, :]
            return (out, new_state)
        return _reference_tuple_inner(x, W_r, W_k, W_v, mu_r, mu_k)[0]
    x = L0_attn_x
    x = x + 0.5 * _L0_ffn_ref(_layernorm(x, axis=-1), L0_ffn_W_r, L0_ffn_W_k, L0_ffn_W_v, L0_ffn_mu_r, L0_ffn_mu_k)
    x = x + _L0_attn_ref(_layernorm(x, axis=-1), L0_attn_Wq, L0_attn_Wk, L0_attn_Wv, L0_attn_Wu, L0_attn_Wo)
    x = x + 0.5 * _L0_ffn_ref(_layernorm(x, axis=-1), L0_ffn_W_r, L0_ffn_W_k, L0_ffn_W_v, L0_ffn_mu_r, L0_ffn_mu_k)
    return x

_drawn_inputs = setup_inputs


def setup_inputs(seed=0):
    import zlib

    import numpy as np

    out = dict(_drawn_inputs(seed))
    spreads = {}
    factors = {'L0_ffn_W_r': 3.453, 'L0_ffn_mu_r': 7.118}
    for name, (base, spread) in spreads.items():
        noise = np.random.default_rng([zlib.crc32(name.encode()), seed]).standard_normal(out[name].shape)
        drawn = base * np.exp(spread * noise) if base else spread * noise
        out[name] = jnp.asarray(drawn.astype(out[name].dtype))
    for name, factor in factors.items():
        out[name] = (out[name] * factor).astype(out[name].dtype)
    return out
```

```python
from contextlib import ExitStack

import concourse.bass as bass
from concourse import mybir

F32 = mybir.dt.float32
F32R = mybir.dt.float32r
I32 = mybir.dt.int32
ALU = mybir.AluOpType
ACT = mybir.ActivationFunctionType
AX_X = mybir.AxisListType.X

P = 128
D = 256
HALVES = D // P
HEAD = 16
TILES = 4
BLOCK = TILES * P
ROW = TILES * D
BANK = 512
LN_EPS = 1e-5
NORM_EPS = 1e-12
RSQRT_MAGIC = 0x5F3759DF
NEWTON_STEPS = 3

WEIGHTS = ("ffn_k", "ffn_r", "ffn_v", "k", "v", "u", "q", "o")
COL = {name: D * n for n, name in enumerate(WEIGHTS)}


def macaron(nc, x, w_t, mu_r, mu_k, out):
    tokens = x.shape[0]
    batches, seq = 2, tokens // 2
    NB = tokens // BLOCK
    BB = seq // BLOCK
    assert x.shape[1] == D and seq % BLOCK == 0 and NB == batches * BB

    with ExitStack() as ctx:
        def sb(name, shape, dt=F32):
            return ctx.enter_context(nc.sbuf_tensor(name, shape, dt))

        def sem(name):
            return ctx.enter_context(nc.semaphore(name))

        xs = sb("xs", [P, NB * ROW])
        silu_u = sb("silu_u", [P, NB * ROW])
        q_store = sb("q_store", [P, NB * HALVES * BLOCK])
        kv_part = sb("kv_part", [P, NB * D])
        w_raw = silu_u[:, 0:len(WEIGHTS) * HALVES * D].rearrange(
            "p (n c e) -> p n c e", n=len(WEIGHTS), c=HALVES)
        w_hi = sb("w_hi", [P, HALVES, len(WEIGHTS) * D], F32R)
        w_lo = sb("w_lo", [P, HALVES, len(WEIGHTS) * D], F32R)
        mu = sb("mu", [P, 2, HALVES])
        one_mu = sb("one_mu", [P, 2, HALVES])
        ident = sb("ident", [P, P])
        head_mask = sb("head_mask", [P, P])
        keep = sb("keep", [P, 2 * NB])
        minus_half = sb("minus_half", [P, TILES])
        zeros = sb("zeros", [P, TILES])
        wait_here = sb("wait_here", [P, 4])
        stats = {k: sb("stats" + k, [P, TILES, 6]) for k in "AB"}
        meanvar = {k: sb("meanvar" + k, [P, TILES, 2]) for k in "AB"}
        var_eps = {k: sb("var_eps" + k, [P, TILES]) for k in "AB"}
        neg_mean = {k: sb("neg_mean" + k, [P, TILES]) for k in "AB"}
        rstd = {k: sb("rstd" + k, [P, TILES]) for k in "AB"}
        shift = {k: sb("shift" + k, [P, TILES]) for k in "AB"}
        kv_bd = sb("kv_bd", [P, NB * D])
        xn = {"A": sb("xnA", [P, TILES, D]),
              "B": kv_bd[:, 0:ROW].rearrange("p (t d) -> p t d", t=TILES)}
        xt = sb("xt", [P, HALVES, 1 + BLOCK])
        mix = sb("mix", [P, 2, HALVES, BLOCK])
        mix_hi = sb("mix_hi", [P, 2, HALVES, BLOCK], F32R)
        mix_lo = sb("mix_lo", [P, 2, HALVES, BLOCK], F32R)
        act_k = sb("act_k", [P, HALVES, BLOCK])
        act_hi = sb("act_hi", [P, HALVES, BLOCK], F32R)
        act_lo = sb("act_lo", [P, HALVES, BLOCK], F32R)
        gate = sb("gate", [P, 2, BANK])
        x2_hi = sb("x2_hi", [P, HALVES, BLOCK], F32R)
        x2_lo = sb("x2_lo", [P, HALVES, BLOCK], F32R)
        k_tok = kv_bd[:, ROW:2 * ROW].rearrange("p (t d) -> p t d", t=TILES)
        v_tok = sb("v_tok", [P, TILES, D])
        kv_sum = v_tok
        q_out = xn["A"][:].rearrange("p t d -> p (t d)")
        q_blk = w_hi[:, 0, COL["k"]:COL["k"] + HALVES * BLOCK].bitcast(F32)
        squares = kv_part[:, 0:ROW].rearrange("p (n e) -> p n e", n=2)
        heads = ROW // HEAD
        head_ss = sb("head_ss", [P, heads])
        head_half = sb("head_half", [P, heads], I32)
        head_rn = sb("head_rn", [P, heads])
        head_y = sb("head_y", [P, heads])
        head_t = sb("head_t", [P, heads])
        scale_u = v_tok[:].rearrange("p t d -> p (t d)")
        gout = kv_part[:, ROW:2 * ROW].rearrange("p (t d) -> p t d", t=TILES)
        g_hi, g_lo = x2_hi, x2_lo

        ps01 = ctx.enter_context(nc.psum_tensor("ps01", [P, 2, BANK], F32))
        ps23 = ctx.enter_context(nc.psum_tensor("ps23", [P, 2, BANK], F32))
        ps45 = ctx.enter_context(nc.psum_tensor("ps45", [P, 2, BANK], F32))
        ps67 = ctx.enter_context(nc.psum_tensor("ps67", [P, 2, BANK], F32))

        s_x_in = sem("s_x_in")
        s_w_in = [sem(f"s_w_in_{n}") for n in WEIGHTS]
        s_mu_in = sem("s_mu_in")
        s_const = sem("s_const")
        s_keep = sem("s_keep")
        s_w_hi = sem("s_w_hi")
        s_w_lo = sem("s_w_lo")
        s_bn = {k: sem("s_bn" + k) for k in "AB"}
        s_mv = {k: sem("s_mv" + k) for k in "AB"}
        s_pool = {k: sem("s_pool" + k) for k in "AB"}
        s_ln = {k: sem("s_ln" + k) for k in "AB"}
        s_xn = {k: sem("s_xn" + k) for k in "AB"}
        s_t = {k: sem("s_t" + k) for k in "AB"}
        s_halo = sem("s_halo")
        s_xt = sem("s_xt")
        s_prev = sem("s_prev")
        s_mix = sem("s_mix")
        s_mix_hi = sem("s_mix_hi")
        s_klo = sem("s_klo")
        s_rlo = sem("s_rlo")
        s_k = sem("s_k")
        s_r = sem("s_r")
        s_relu_k = sem("s_relu_k")
        s_act_k = sem("s_act_k")
        s_act_hi = sem("s_act_hi")
        s_act_lo = sem("s_act_lo")
        s_gate = sem("s_gate")
        s_f = sem("s_f")
        s_gated = sem("s_gated")
        s_x1 = sem("s_x1")
        s_x2_hi = sem("s_x2_hi")
        s_x2_lo = sem("s_x2_lo")
        s_kv = sem("s_kv")
        s_kv_tok = sem("s_kv_tok")
        s_u = sem("s_u")
        s_sig_u = sem("s_sig_u")
        s_silu = sem("s_silu")
        s_q = sem("s_q")
        s_q_blk = sem("s_q_blk")
        s_q_saved = sem("s_q_saved")
        s_kvs = sem("s_kvs")
        s_kv_part = sem("s_kv_part")
        s_sum = sem("s_sum")
        s_kv_bd = sem("s_kv_bd")
        s_q_back = sem("s_q_back")
        s_o = sem("s_o")
        s_sq = sem("s_sq")
        s_ss = sem("s_ss")
        s_newton = sem("s_newton")
        s_rn = sem("s_rn")
        s_scale_u = sem("s_scale_u")
        s_gout = sem("s_gout")
        s_gt = sem("s_gt")
        s_g_hi = sem("s_g_hi")
        s_g_lo = sem("s_g_lo")
        s_wo = sem("s_wo")
        s_x2 = sem("s_x2")
        s_x3 = sem("s_x3")
        s_out = sem("s_out")

        NEWTON_OPS = 3 + 3 * NEWTON_STEPS - 1

        def row(tile, block, start=0, n=ROW):
            return tile[:, bass.ds(block * ROW + start, n)]

        block = ctx.enter_context(nc.Block())

        @block.sync
        def _(sp):
            def load_x(b):
                sp.dma_start(row(xs, b).rearrange("p (t d) -> p t d", t=TILES),
                             x[bass.ds(b * BLOCK, BLOCK), :].rearrange("(t p) d -> p t d", p=P)
                             ).then_inc(s_x_in, 16)
                sp.wait_ge(s_x_in, (b + 1) * 16)

            def save_q(a):
                sp.wait_ge(s_q_blk, (a + 1) * HALVES)
                sp.dma_start(row(q_store, a), q_out).then_inc(s_q_saved, 16)

            def load_q(j):
                if j == 0:
                    sp.wait_ge(s_q_saved, 16 * NB)
                else:
                    sp.wait_ge(s_o, j * 2)
                sp.dma_start(q_blk, row(q_store, j)).then_inc(s_q_back, 16)

            def store_x(b):
                sp.wait_ge(s_x3, (b + 1) * 2)
                sp.dma_start(out[bass.ds(b * BLOCK, BLOCK), :].rearrange("(t p) d -> p t d", p=P),
                             row(xs, b).rearrange("p (t d) -> p t d", t=TILES)).then_inc(s_out, 16)

            for b in range(NB):
                load_x(b)
            for a in range(NB):
                save_q(a)
            for j in range(3):
                load_q(j)
            for j in range(3, NB):
                load_q(j)
                store_x(j - 3)
            for b in range(NB - 3, NB):
                store_x(b)
            sp.wait_ge(s_out, 16 * NB)

        @block.gpsimd
        def _(pool):
            nc.gpsimd.memset(ident[:], 0.0).then_inc(s_const, 1)
            nc.gpsimd.memset(head_mask[:], 1.0 / HEAD).then_inc(s_const, 1)
            nc.gpsimd.memset(minus_half[:], -0.5).then_inc(s_const, 1)
            nc.gpsimd.memset(zeros[:], 0.0).then_inc(s_const, 1)
            pool.wait_ge(s_const, 4)
            nc.gpsimd.affine_select(out=ident[:], in_=ident[:], compare_op=ALU.not_equal, fill=1.0, base=0,
                                    pattern=[[-1, P]], channel_multiplier=1).then_inc(s_const, 1)
            by_head = head_mask[:].rearrange("p (h e) -> p h e", e=HEAD)
            nc.gpsimd.affine_select(out=by_head, in_=by_head, compare_op=ALU.is_ge, fill=0.0, base=0,
                                    pattern=[[-HEAD, P // HEAD], [0, HEAD]],
                                    channel_multiplier=1).then_inc(s_const, 1)
            pool.wait_ge(s_const, 6)
            nc.gpsimd.affine_select(out=by_head, in_=by_head, compare_op=ALU.is_ge, fill=0.0, base=HEAD - 1,
                                    pattern=[[HEAD, P // HEAD], [0, HEAD]],
                                    channel_multiplier=-1).then_inc(s_const, 1)

            def ln_scales(kind, n, first=False):
                pool.wait_ge(s_mv[kind], (n + 1) * TILES)
                nc.gpsimd.tensor_tensor(neg_mean[kind][:], zeros[:], meanvar[kind][:, :, 0],
                                        ALU.subtract).then_inc(s_pool[kind], 1)
                nc.gpsimd.tensor_scalar(var_eps[kind][:], meanvar[kind][:, :, 1], 1.0, LN_EPS,
                                        ALU.mult, ALU.add).then_inc(s_pool[kind], 1)
                pool.wait_ge(s_pool[kind], (n + 1) * 2)
                if not first:
                    pool.wait_ge(s_xn[kind], n * TILES)
                nc.gpsimd.tensor_tensor(rstd[kind][:], var_eps[kind][:], minus_half[:],
                                        ALU.pow).then_inc(s_ln[kind], 1)
                pool.wait_ge(s_ln[kind], n * 2 + 1)
                nc.gpsimd.tensor_tensor(shift[kind][:], neg_mean[kind][:], rstd[kind][:],
                                        ALU.mult).then_inc(s_ln[kind], 1)

            def mix_low(rk, f, s_low, s_used, first=False):
                for h in range(HALVES):
                    pool.wait_ge(s_mix_hi, f * 4 + rk * 2 + h + 1)
                    if not first and h == 0:
                        pool.wait_ge(s_used, f * 2)
                    nc.gpsimd.tensor_tensor(mix_lo[:, rk, h, :], mix[:, rk, h, :],
                                            mix_hi[:, rk, h, :].bitcast(F32),
                                            ALU.subtract).then_inc(s_low, 1)

            def square_k(f):
                for h in range(HALVES):
                    pool.wait_ge(s_act_hi, f * 2 + h + 1)
                    nc.gpsimd.tensor_tensor(act_k[:, h, :], act_k[:, h, :], act_k[:, h, :],
                                            ALU.mult).then_inc(s_act_k, 1)

            def act_low(f, first=False):
                for h in range(HALVES):
                    pool.wait_ge(s_act_k, f * 2 + h + 1)
                    if not first and h == 0:
                        pool.wait_ge(s_f, f * 2)
                    nc.gpsimd.tensor_tensor(act_lo[:, h, :], act_k[:, h, :],
                                            act_hi[:, h, :].bitcast(F32), ALU.subtract).then_inc(s_act_lo, 1)

            def scale_gate(j, first=False):
                pool.wait_ge(s_rn, j + 1)
                if not first:
                    pool.wait_ge(s_gout, j * 2)
                nc.gpsimd.tensor_tensor(scale_u[:].rearrange("p (n e) -> p n e", e=HEAD),
                                        row(silu_u, j).rearrange("p (n e) -> p n e", e=HEAD),
                                        head_rn[:].unsqueeze(2).to_broadcast([P, heads, HEAD]),
                                        ALU.mult).then_inc(s_scale_u, 1)

            def add_ffn2(f):
                b = f - NB
                for n in range(2):
                    pool.wait_ge(s_gated, f * 2 + n + 1)
                    xb = row(xs, b, n * BANK, BANK)
                    nc.gpsimd.tensor_tensor(xb, xb, gate[:, n, :], ALU.add).then_inc(s_x3, 1)

            ln_scales("A", 0, first=True)
            mix_low(1, 0, s_rlo, s_r, first=True)
            ln_scales("A", 1)
            square_k(0)
            act_low(0, first=True)
            mix_low(1, 1, s_rlo, s_r)
            ln_scales("B", 0, first=True)
            with pool.Fori(1, NB - 1) as i:
                square_k(i)
                ln_scales("A", i + 1)
                act_low(i)
                mix_low(1, i + 1, s_rlo, s_r)
                ln_scales("B", i)
            square_k(NB - 1)
            act_low(NB - 1)
            ln_scales("B", NB - 1)
            scale_gate(0, first=True)
            scale_gate(1)
            ln_scales("A", NB)
            mix_low(0, NB, s_klo, s_k)
            mix_low(1, NB, s_rlo, s_r)
            with pool.Fori(2, NB) as j:
                scale_gate(j)
                ln_scales("A", j + (NB - 1))
                mix_low(0, j + (NB - 1), s_klo, s_k)
                mix_low(1, j + (NB - 1), s_rlo, s_r)
                add_ffn2(j + (NB - 2))
            ln_scales("A", 2 * NB - 1)
            mix_low(0, 2 * NB - 1, s_klo, s_k)
            mix_low(1, 2 * NB - 1, s_rlo, s_r)
            add_ffn2(2 * NB - 2)
            add_ffn2(2 * NB - 1)

        @block.scalar
        def _(act):
            for n, name in enumerate(WEIGHTS):
                act.dma_start(w_raw[:, n, :, :], w_t[name].rearrange("(c p) e -> p c e", p=P)
                              ).then_inc(s_w_in[n], 16)
                if n == 0:
                    act.dma_start(mu[:, 0, :], mu_k).then_inc(s_mu_in, 16)
                    act.dma_start(mu[:, 1, :], mu_r).then_inc(s_mu_in, 16)

            def split_weights(lo, hi):
                for n in range(lo, hi):
                    act.wait_ge(s_w_in[n], 16)
                    cols = slice(n * D, (n + 1) * D)
                    nc.scalar.activation(w_hi[:, :, cols], w_raw[:, n, :, :], ACT.Identity,
                                         scale=0.5 if WEIGHTS[n] == "ffn_v" else 1.0).then_inc(s_w_hi, 1)

            def normalize(kind, n, b, first=False, q_saved=0):
                act.wait_ge(s_ln[kind], (n + 1) * 2)
                if not first:
                    act.wait_ge(s_t[kind], n * HALVES)
                if isinstance(q_saved, int) and q_saved == 0:
                    pass
                else:
                    act.wait_ge(s_q_saved, q_saved * 16)
                for t in range(TILES):
                    nc.scalar.activation(xn[kind][:, t, :], row(xs, b, t * D, D), ACT.Identity,
                                         bias=shift[kind][:, t:t + 1],
                                         scale=rstd[kind][:, t:t + 1]).then_inc(s_xn[kind], 1)

            def mix_previous(f, first=False):
                if first:
                    act.wait_ge(s_keep, 3)
                    act.wait_ge(s_keep, 3)
                else:
                    act.wait_ge(s_mix, f * 4)
                    nc.scalar.activation(xt[:, :, 0:1], xt[:, :, BLOCK:BLOCK + 1], ACT.Copy,
                                         scale=keep[:, bass.ds(f, 1)]).then_inc(s_halo, 1)
                    act.wait_ge(s_halo, f * 1)
                for h in range(HALVES):
                    act.wait_ge(s_t["A"], f * 2 + h + 1)
                    nc.scalar.activation(xt[:, h, 1:1 + BLOCK], ps23[:, h, :], ACT.Identity).then_inc(s_xt, 1)
                if not first:
                    act.wait_ge(s_klo, f * 2)
                    act.wait_ge(s_rlo, f * 2)
                for rk in range(2):
                    for h in range(HALVES):
                        act.wait_ge(s_xt, f * 2 + h + 1)
                        nc.scalar.activation(mix[:, rk, h, :], xt[:, h, 0:BLOCK], ACT.Copy,
                                             scale=one_mu[:, rk, h:h + 1]).then_inc(s_prev, 1)

            def mix_high(f, first=False):
                for rk in range(2):
                    if not first:
                        act.wait_ge((s_k, s_r)[rk], f * 2)
                    for h in range(HALVES):
                        act.wait_ge(s_mix, f * 4 + rk * 2 + h + 1)
                        nc.scalar.activation(mix_hi[:, rk, h, :], mix[:, rk, h, :],
                                             ACT.Identity).then_inc(s_mix_hi, 1)

            def relu_k(f, h):
                act.wait_ge(s_k, f * 2 + h + 1)
                nc.scalar.activation(act_k[:, h, :], ps23[:, h, :], ACT.Relu).then_inc(s_relu_k, 1)

            def square_high(f, h):
                act.wait_ge(s_relu_k, f * 2 + h + 1)
                nc.scalar.activation(act_hi[:, h, :], act_k[:, h, :], ACT.Square).then_inc(s_act_hi, 1)

            def activate_k(f, first=False, square=False):
                if not first:
                    act.wait_ge(s_act_lo, f * 2)
                relu_k(f, 0)
                if not first:
                    act.wait_ge(s_f, f * 2)
                square_high(f, 0)
                relu_k(f, 1)
                square_high(f, 1)
                if square:
                    for h in range(HALVES):
                        nc.scalar.activation(act_k[:, h, :], act_k[:, h, :], ACT.Square).then_inc(s_act_k, 1)

            def sigmoid_r(f, s_added=None, added=0):
                for n in range(2):
                    act.wait_ge(s_r, f * 2 + n + 1)
                    if s_added is not None and n == 0:
                        act.wait_ge(s_added, added)
                    nc.scalar.activation(gate[:, n, :], ps45[:, n, :], ACT.Sigmoid).then_inc(s_gate, 1)

            def high_of(ps, hi, a, s_from, s_to, s_used, used):
                for h in range(HALVES):
                    act.wait_ge(s_from, a * 2 + h + 1)
                    if used is not None and h == 0:
                        act.wait_ge(s_used, used)
                    nc.scalar.activation(hi[:, h, :], ps[:, h, :], ACT.Identity).then_inc(s_to, 1)

            def sigmoid_u(a, first=False):
                for n in range(2):
                    act.wait_ge(s_u, a * 2 + n + 1)
                    if first and n == 0:
                        act.wait_ge(s_w_lo, len(WEIGHTS))
                    nc.scalar.activation(row(silu_u, a, n * BANK, BANK), ps01[:, n, :], ACT.Sigmoid).then_inc(s_sig_u, 1)

            def relu_q(a, ln_used, first=False):
                for h in range(HALVES):
                    act.wait_ge(s_q, a * 2 + h + 1)
                    if h == 0:
                        act.wait_ge(s_t["A"], ln_used * 2)
                        if not first:
                            act.wait_ge(s_q_saved, a * 16)
                    nc.scalar.activation(q_out[:, h * BLOCK:(h + 1) * BLOCK], ps67[:, h, :],
                                         ACT.Relu).then_inc(s_q_blk, 1)

            def square_heads(j, first=False):
                for n in range(2):
                    act.wait_ge(s_o, j * 2 + n + 1)
                    if not first and n == 0:
                        act.wait_ge(s_ss, j * 2)
                    nc.scalar.activation(squares[:, n, :], ps67[:, n, :], ACT.Square,
                                         scale=float(HEAD) ** -0.5).then_inc(s_sq, 1)

            def x2_high(a, first=False):
                high_of(ps01, x2_hi, a, s_t["B"], s_x2_hi, s_q, None if first else a * 2)

            def g_high(j, first=False):
                high_of(ps67, g_hi, j, s_gt, s_g_hi, s_wo, None if first else j * 2)

            split_weights(0, 2)
            normalize("A", 0, 0, first=True)
            mix_previous(0, first=True)
            mix_high(0, first=True)
            split_weights(2, len(WEIGHTS))
            normalize("A", 1, 1)
            activate_k(0, first=True)
            sigmoid_r(0)
            mix_previous(1)
            mix_high(1)

            def phase1(i, first=False, last=False):
                activate_k(i)
                normalize("B", i - 1, i - 1, first=first)
                x2_high(i - 1, first=first)
                sigmoid_r(i, s_x1, i * 2)
                if not last:
                    normalize("A", i + 1, i + 1, q_saved=0 if first else i - 1)
                    mix_previous(i + 1)
                sigmoid_u(i - 1, first=first)
                if not last:
                    mix_high(i + 1)
                relu_q(i - 1, i + (1 if last else 2), first=first)

            phase1(1, first=True)
            with act.Fori(2, NB - 1) as i:
                phase1(i)
            phase1(NB - 1, last=True)
            normalize("B", NB - 1, NB - 1)
            x2_high(NB - 1)
            sigmoid_u(NB - 1)
            relu_q(NB - 1, NB)
            square_heads(0, first=True)
            g_high(0, first=True)
            square_heads(1)
            normalize("A", NB, 0, q_saved=NB)
            g_high(1)
            mix_previous(NB)
            mix_high(NB)

            def phase2(j, s_added, added):
                square_heads(j)
                activate_k(j + (NB - 2), square=True)
                normalize("A", j + (NB - 1), j - 1)
                sigmoid_r(j + (NB - 2), s_added, added)
                g_high(j)
                mix_previous(j + (NB - 1))
                mix_high(j + (NB - 1))

            phase2(2, s_x1, 2 * NB)
            with act.Fori(3, NB) as j:
                phase2(j, s_x3, (j - 2) * 2)
            normalize("A", 2 * NB - 1, NB - 1)
            activate_k(2 * NB - 2, square=True)
            sigmoid_r(2 * NB - 2, s_x3, 2 * (NB - 2))
            mix_previous(2 * NB - 1)
            mix_high(2 * NB - 1)
            activate_k(2 * NB - 1, square=True)
            sigmoid_r(2 * NB - 1, s_x3, 2 * (NB - 1))

        @block.vector
        def _(dve):
            nc.vector.memset(keep[:], 1.0).then_inc(s_keep, 1)
            nc.vector.memset(xt[:, :, 0:1], 0.0).then_inc(s_keep, 1)
            dve.wait_ge(s_keep, 2)
            nc.vector.memset(keep[:, 0:2 * NB:BB], 0.0).then_inc(s_keep, 1)
            dve.wait_ge(s_mu_in, 32)
            nc.vector.tensor_scalar(one_mu[:], mu[:], -1.0, 1.0, ALU.mult, ALU.add).then_inc(s_keep, 1)

            def split_weights(lo, hi):
                for n in range(lo, hi):
                    dve.wait_ge(s_w_hi, n + 1)
                    cols = slice(n * D, (n + 1) * D)
                    nc.vector.scalar_tensor_tensor(
                        out=w_lo[:, :, cols], in0=w_raw[:, n, :, :],
                        scalar=0.5 if WEIGHTS[n] == "ffn_v" else 1.0,
                        in1=w_hi[:, :, cols].bitcast(F32), op0=ALU.mult, op1=ALU.subtract).then_inc(s_w_lo, 1)

            def ln_stats(kind, n, b, first=False):
                col = 2 * "AB".index(kind)
                nc.vector.memset(wait_here[:, col:col + 1], 0.0)
                for t in range(TILES):
                    nc.vector.bn_stats(stats[kind][:, t, :], row(xs, b, t * D, D)).then_inc(s_bn[kind], 1)
                if not first:
                    dve.wait_ge(s_ln[kind], n * 2)
                dve.wait_ge(s_bn[kind], (n + 1) * TILES)
                nc.vector.memset(wait_here[:, col + 1:col + 2], 0.0)
                for t in range(TILES):
                    nc.vector.bn_aggr(meanvar[kind][:, t, :], stats[kind][:, t, :]).then_inc(s_mv[kind], 1)

            def mix_current(rk, f):
                for h in range(HALVES):
                    dve.wait_ge(s_prev, f * 4 + rk * 2 + h + 1)
                    m = mix[:, rk, h, :]
                    nc.vector.scalar_tensor_tensor(out=m, in0=xt[:, h, 1:1 + BLOCK], scalar=mu[:, rk, h:h + 1],
                                                   in1=m, op0=ALU.mult, op1=ALU.add).then_inc(s_mix, 1)

            def k_mix_low(f, first=False):
                for h in range(HALVES):
                    dve.wait_ge(s_mix_hi, f * 4 + h + 1)
                    if not first and h == 0:
                        dve.wait_ge(s_k, f * 2)
                    nc.vector.tensor_tensor(mix_lo[:, 0, h, :], mix[:, 0, h, :],
                                            mix_hi[:, 0, h, :].bitcast(F32), ALU.subtract).then_inc(s_klo, 1)

            def act_low(f, first=False):
                for h in range(HALVES):
                    dve.wait_ge(s_act_k, f * 2 + h + 1)
                    dve.wait_ge(s_act_hi, f * 2 + h + 1)
                    if not first and h == 0:
                        dve.wait_ge(s_f, f * 2)
                    nc.vector.tensor_tensor(act_lo[:, h, :], act_k[:, h, :],
                                            act_hi[:, h, :].bitcast(F32), ALU.subtract).then_inc(s_act_lo, 1)

            def gate_ffn(f):
                for n in range(2):
                    dve.wait_ge(s_f, f * 2 + n + 1)
                    dve.wait_ge(s_gate, f * 2 + n + 1)
                    nc.vector.tensor_tensor(gate[:, n, :], ps45[:, n, :], gate[:, n, :],
                                            ALU.mult).then_inc(s_gated, 1)

            def add_ffn1(f):
                for n in range(2):
                    dve.wait_ge(s_gated, f * 2 + n + 1)
                    xb = row(xs, f, n * BANK, BANK)
                    nc.vector.tensor_tensor(xb, xb, gate[:, n, :], ALU.add).then_inc(s_x1, 1)

            def low_of(ps, hi, lo, a, s_from, s_to):
                for h in range(HALVES):
                    dve.wait_ge(s_from, a * 2 + h + 1)
                    nc.vector.tensor_tensor(lo[:, h, :], ps[:, h, :], hi[:, h, :].bitcast(F32),
                                            ALU.subtract).then_inc(s_to, 1)

            def keep_kv(a, first=False):
                for t in range(TILES):
                    dve.wait_ge(s_kv, a * TILES + t + 1)
                    if not first and t == 0:
                        dve.wait_ge(s_kvs, a * 1)
                    nc.vector.tensor_copy(v_tok[:, t, :], ps67[:, t % 2, D:2 * D]).then_inc(s_kv_tok, 1)
                    nc.vector.tensor_scalar(k_tok[:, t, :], ps67[:, t % 2, 0:D], 0.0, None,
                                            ALU.max).then_inc(s_kv_tok, 1)

            def silu(a):
                for n in range(2):
                    dve.wait_ge(s_sig_u, a * 2 + n + 1)
                    su = row(silu_u, a, n * BANK, BANK)
                    nc.vector.tensor_tensor(su, ps01[:, n, :], su, ALU.mult).then_inc(s_silu, 1)

            def keep_kv_part(a):
                dve.wait_ge(s_kvs, a + 1)
                nc.vector.tensor_copy(kv_part[:, bass.ds(a * D, D)], ps01[:, 0, 0:D]).then_inc(s_kv_part, 1)

            def sum_kv(batch):
                first = batch * BB
                dve.wait_ge(s_kv_part, first + BB)
                for n in range(1, BB):
                    a = kv_part[:, first * D:(first + 1) * D] if n == 1 else kv_sum[:, batch, :]
                    if n > 1:
                        dve.wait_ge(s_sum, batch * (BB - 1) + n - 1)
                    nc.vector.tensor_tensor(kv_sum[:, batch, :], a, kv_part[:, (first + n) * D:(first + n + 1) * D],
                                            ALU.add).then_inc(s_sum, 1)
                dve.wait_ge(s_sum, (batch + 1) * (BB - 1))
                dve.wait_ge(s_const, 7)
                for n in range(BB):
                    nc.vector.tensor_tensor(
                        kv_bd[:, (first + n) * D:(first + n + 1) * D].rearrange("p (h e) -> p h e", h=HALVES),
                        kv_sum[:, batch, :].rearrange("p (h e) -> p h e", h=HALVES),
                        head_mask[:].unsqueeze(1).to_broadcast([P, HALVES, P]), ALU.mult).then_inc(s_kv_bd, 1)

            def add_attention(j, n):
                dve.wait_ge(s_wo, j * 2 + n + 1)
                xb = row(xs, j, n * BANK, BANK)
                nc.vector.tensor_tensor(xb, xb, ps01[:, n, :], ALU.add).then_inc(s_x2, 1)

            def head_norms(j, attention_of=None, first=False):
                for n in range(2):
                    dve.wait_ge(s_sq, j * 2 + n + 1)
                    nc.vector.tensor_reduce(head_ss[:, n * heads // 2:(n + 1) * heads // 2],
                                            squares[:, n, :].rearrange("p (g e) -> p g e", e=HEAD),
                                            AX_X, ALU.add).then_inc(s_ss, 1)
                dve.wait_ge(s_ss, (j + 1) * 2)
                step = [0]

                def then(ins, meanwhile=None):
                    step[0] += 1
                    ins.then_inc(s_newton, 1)
                    if meanwhile is not None:
                        meanwhile()
                    dve.wait_ge(s_newton, j * NEWTON_OPS + step[0])

                then(nc.vector.tensor_scalar(head_ss[:], head_ss[:], NORM_EPS ** 2, None, ALU.max))
                then(nc.vector.tensor_scalar(head_half[:], head_ss[:].bitcast(I32), 1, None,
                                             ALU.arith_shift_right))
                then(nc.vector.tensor_scalar(head_y[:].bitcast(I32), head_half[:], -1.0, float(RSQRT_MAGIC),
                                             ALU.mult, ALU.add))
                if not first:
                    dve.wait_ge(s_scale_u, j * 1)
                for n in range(NEWTON_STEPS):
                    last = n == NEWTON_STEPS - 1
                    then(nc.vector.tensor_tensor(head_t[:], head_y[:], head_y[:], ALU.mult))
                    then(nc.vector.scalar_tensor_tensor(out=head_t[:], in0=head_t[:], scalar=-0.5,
                                                        in1=head_ss[:], op0=ALU.mult, op1=ALU.mult))
                    y = nc.vector.scalar_tensor_tensor(out=head_rn[:] if last else head_y[:], in0=head_t[:],
                                                       scalar=1.5, in1=head_y[:], op0=ALU.add, op1=ALU.mult)
                    if last:
                        y.then_inc(s_rn, 1)
                    elif not first and attention_of is not None:
                        then(y, lambda: add_attention(attention_of, n))
                    else:
                        then(y)
                assert step[0] == NEWTON_OPS

            def gate_heads(j, first=False):
                dve.wait_ge(s_scale_u, j + 1)
                if not first:
                    dve.wait_ge(s_gt, j * 2)
                for n in range(2):
                    nc.vector.tensor_tensor(gout[:, 2 * n:2 * n + 2, :],
                                            ps67[:, n, :].rearrange("p (t d) -> p t d", t=2),
                                            scale_u[:, n * BANK:(n + 1) * BANK].rearrange("p (t d) -> p t d", t=2),
                                            ALU.mult).then_inc(s_gout, 1)

            def stats_of_input(f, first=False):
                dve.wait_ge(s_x_in, (f + 1) * 16)
                ln_stats("A", f, f, first=first)

            def stats_of_x1(a, first=False):
                dve.wait_ge(s_x1, (a + 1) * 2)
                ln_stats("B", a, a, first=first)

            def stats_of_x2(f, b):
                dve.wait_ge(s_x2, (b + 1) * 2)
                ln_stats("A", f, b)

            stats_of_input(0, first=True)
            split_weights(0, 2)
            dve.wait_ge(s_keep, 4)
            mix_current(0, 0)
            k_mix_low(0, first=True)
            mix_current(1, 0)
            split_weights(2, len(WEIGHTS))
            stats_of_input(1)
            mix_current(0, 1)
            k_mix_low(1)
            mix_current(1, 1)
            gate_ffn(0)
            add_ffn1(0)
            stats_of_x1(0, first=True)

            def phase1(i, first=False, last=False):
                if not last:
                    stats_of_input(i + 1)
                low_of(ps01, x2_hi, x2_lo, i - 1, s_x2_hi, s_x2_lo)
                keep_kv(i - 1, first=first)
                if not last:
                    mix_current(0, i + 1)
                    mix_current(1, i + 1)
                silu(i - 1)
                if not last:
                    k_mix_low(i + 1)
                gate_ffn(i)
                add_ffn1(i)
                stats_of_x1(i)
                keep_kv_part(i - 1)

            phase1(1, first=True)
            with dve.Fori(2, NB - 1) as i:
                phase1(i)
            phase1(NB - 1, last=True)
            low_of(ps01, x2_hi, x2_lo, NB - 1, s_x2_hi, s_x2_lo)
            keep_kv(NB - 1)
            silu(NB - 1)
            keep_kv_part(NB - 1)
            sum_kv(0)
            sum_kv(1)
            head_norms(0, first=True)
            gate_heads(0, first=True)
            low_of(ps67, g_hi, g_lo, 0, s_g_hi, s_g_lo)
            head_norms(1, attention_of=0)
            stats_of_x2(NB, 0)
            gate_heads(1)
            low_of(ps67, g_hi, g_lo, 1, s_g_hi, s_g_lo)
            mix_current(0, NB)
            mix_current(1, NB)

            def phase2(j):
                head_norms(j, attention_of=j - 1)
                stats_of_x2(j + (NB - 1), j - 1)
                gate_heads(j)
                act_low(j + (NB - 2))
                low_of(ps67, g_hi, g_lo, j, s_g_hi, s_g_lo)
                mix_current(0, j + (NB - 1))
                mix_current(1, j + (NB - 1))
                gate_ffn(j + (NB - 2))

            with dve.Fori(2, NB) as j:
                phase2(j)
            for n in range(2):
                add_attention(NB - 1, n)
            stats_of_x2(2 * NB - 1, NB - 1)
            act_low(2 * NB - 2)
            mix_current(0, 2 * NB - 1)
            mix_current(1, 2 * NB - 1)
            gate_ffn(2 * NB - 2)
            act_low(2 * NB - 1)
            gate_ffn(2 * NB - 1)

        @block.tensor
        def _(pe):
            def product(dst, a_hi, a_lo, b_hi, b_lo, start, stop):
                nc.tensor.matmul(dst, a_hi, b_hi, start=start, stop=False)
                nc.tensor.matmul(dst, a_hi, b_lo, start=False, stop=False)
                return nc.tensor.matmul(dst, a_lo, b_hi, start=False, stop=stop)

            def weight(name, c, start=0, n=D):
                cols = slice(COL[name] + start, COL[name] + start + n)
                return w_hi[:, c, cols], w_lo[:, c, cols]

            def token_rows(hi, lo, c, t):
                cols = slice(t * P, (t + 1) * P)
                return hi[:, c, cols], lo[:, c, cols]

            def to_features(kind, n, ps):
                for h in range(HALVES):
                    for t in range(TILES):
                        if h == 0:
                            pe.wait_ge(s_xn[kind], n * TILES + t + 1)
                        last = nc.tensor.transpose(ps[:, h, t * P:(t + 1) * P],
                                                   xn[kind][:, t, h * P:(h + 1) * P], ident[:])
                    last.then_inc(s_t[kind], 1)

            def transpose_a(f, first=False):
                if not first:
                    pe.wait_ge(s_relu_k, f * 2)
                to_features("A", f, ps23)

            def ffn_k(f):
                for m in range(HALVES):
                    for c in range(HALVES):
                        if m == 0:
                            pe.wait_ge(s_mix_hi, f * 4 + c + 1)
                            pe.wait_ge(s_klo, f * 2 + c + 1)
                        last = product(ps23[:, m, :], *weight("ffn_k", c, m * P, P),
                                       mix_hi[:, 0, c, :], mix_lo[:, 0, c, :], c == 0, c == HALVES - 1)
                    last.then_inc(s_k, 1)

            def by_tiles(ps, hi, lo, name, s_done):
                for t in range(TILES):
                    for c in range(HALVES):
                        last = product(ps[:, t // 2, (t % 2) * D:(t % 2 + 1) * D], *token_rows(hi, lo, c, t),
                                       *weight(name, c), c == 0, c == HALVES - 1)
                    if t % 2:
                        last.then_inc(s_done, 1)

            def ffn_r(f, first=False):
                pe.wait_ge(s_mix_hi, f * 4 + 4)
                pe.wait_ge(s_rlo, f * 2 + 2)
                if not first:
                    pe.wait_ge(s_gated, f * 2)
                by_tiles(ps45, mix_hi[:, 1, :, :], mix_lo[:, 1, :, :], "ffn_r", s_r)

            def ffn_v(f):
                pe.wait_ge(s_act_hi, f * 2 + 2)
                pe.wait_ge(s_act_lo, f * 2 + 2)
                pe.wait_ge(s_gate, f * 2 + 2)
                by_tiles(ps45, act_hi, act_lo, "ffn_v", s_f)

            def transpose_b(a, first=False):
                if not first:
                    pe.wait_ge(s_kv_part, a * 1)
                    pe.wait_ge(s_silu, a * 2)
                to_features("B", a, ps01)

            def kv_of_tokens(a, first=False):
                pe.wait_ge(s_x2_hi, a * 2 + 2)
                pe.wait_ge(s_x2_lo, a * 2 + 2)
                if not first:
                    pe.wait_ge(s_q_blk, a * 2)
                for t in range(TILES):
                    if t >= 2:
                        pe.wait_ge(s_kv_tok, a * 8 + 2 * (t - 1))
                    for c in range(HALVES):
                        last = product(ps67[:, t % 2, :], *token_rows(x2_hi, x2_lo, c, t),
                                       *weight("k", c, 0, 2 * D), c == 0, c == HALVES - 1)
                    last.then_inc(s_kv, 1)

            def u_of_tokens(a):
                by_tiles(ps01, x2_hi, x2_lo, "u", s_u)

            def q_of_tokens(a):
                pe.wait_ge(s_kv_tok, a * 8 + 8)
                for m in range(HALVES):
                    for c in range(HALVES):
                        last = product(ps67[:, m, :], *weight("q", c, m * P, P),
                                       x2_hi[:, c, :], x2_lo[:, c, :], c == 0, c == HALVES - 1)
                    last.then_inc(s_q, 1)

            def sum_kv_of_block(a):
                pe.wait_ge(s_kv_tok, a * 8 + 8)
                pe.wait_ge(s_silu, a * 2 + 1)
                for h in range(HALVES):
                    half = slice(h * P, (h + 1) * P)
                    for t in range(TILES):
                        last = nc.tensor.matmul(ps01[:, 0, half], k_tok[:, t, half], v_tok[:, t, half],
                                                start=(t == 0), stop=(t == TILES - 1))
                last.then_inc(s_kvs, 1)

            def attend(j, kv_ready, first=False):
                pe.wait_ge(s_q_back, (j + 1) * 16)
                pe.wait_ge(s_kv_bd, kv_ready)
                if not first:
                    pe.wait_ge(s_g_lo, j * 2)
                for t in range(TILES):
                    for h in range(HALVES):
                        last = nc.tensor.matmul(
                            ps67[:, t // 2, (t % 2) * D + h * P:(t % 2) * D + (h + 1) * P],
                            q_blk[:, h * BLOCK + t * P:h * BLOCK + (t + 1) * P],
                            kv_bd[:, bass.ds(j * D + h * P, P)], start=True, stop=True)
                    if t % 2:
                        last.then_inc(s_o, 1)

            def transpose_g(j):
                pe.wait_ge(s_gout, j * 2 + 2)
                for h in range(HALVES):
                    for t in range(TILES):
                        last = nc.tensor.transpose(ps67[:, h, t * P:(t + 1) * P],
                                                   gout[:, t, h * P:(h + 1) * P], ident[:])
                    last.then_inc(s_gt, 1)

            def project_out(j, first=False):
                pe.wait_ge(s_g_hi, j * 2 + 2)
                pe.wait_ge(s_g_lo, j * 2 + 2)
                if not first:
                    pe.wait_ge(s_x2, j * 2)
                by_tiles(ps01, g_hi, g_lo, "o", s_wo)

            pe.wait_ge(s_const, 7)
            transpose_a(0, first=True)
            pe.wait_ge(s_w_lo, 2)
            ffn_k(0)
            ffn_r(0, first=True)
            transpose_a(1)
            pe.wait_ge(s_w_lo, len(WEIGHTS))
            ffn_v(0)

            def phase1(i, first=False, last=False):
                ffn_k(i)
                ffn_r(i)
                transpose_b(i - 1, first=first)
                kv_of_tokens(i - 1, first=first)
                if not last:
                    transpose_a(i + 1)
                u_of_tokens(i - 1)
                ffn_v(i)
                q_of_tokens(i - 1)
                sum_kv_of_block(i - 1)

            phase1(1, first=True)
            with pe.Fori(2, NB - 1) as i:
                phase1(i)
            phase1(NB - 1, last=True)
            transpose_b(NB - 1)
            kv_of_tokens(NB - 1)
            u_of_tokens(NB - 1)
            q_of_tokens(NB - 1)
            sum_kv_of_block(NB - 1)
            pe.wait_ge(s_q_blk, 2 * NB)
            attend(0, NB, first=True)
            transpose_g(0)
            attend(1, NB)
            pe.wait_ge(s_kv_part, NB)
            pe.wait_ge(s_silu, 2 * NB)
            project_out(0, first=True)
            transpose_g(1)
            transpose_a(NB)
            with pe.Fori(2, NB) as j:
                attend(j, NB)
                project_out(j - 1)
                ffn_k(j + (NB - 2))
                ffn_r(j + (NB - 2))
                transpose_g(j)
                transpose_a(j + (NB - 1))
                ffn_v(j + (NB - 2))
            project_out(NB - 1)
            ffn_k(2 * NB - 2)
            ffn_r(2 * NB - 2)
            transpose_a(2 * NB - 1)
            ffn_v(2 * NB - 2)
            ffn_k(2 * NB - 1)
            ffn_r(2 * NB - 1)
            ffn_v(2 * NB - 1)


_W = {"ffn_k": "L0_ffn_W_k", "ffn_r": "L0_ffn_W_r", "ffn_v": "L0_ffn_W_v", "k": "L0_attn_Wk",
      "v": "L0_attn_Wv", "u": "L0_attn_Wu", "q": "L0_attn_Wq", "o": "L0_attn_Wo"}


def kernel(**inputs):
    import numpy as np
    import concourse.bacc as bacc
    from concourse.bass_utils import run_bass_kernel_spmd

    nc = bacc.Bacc("TRN2", target_bir_lowering=False, num_devices=1)
    x = np.asarray(inputs["L0_attn_x"])
    arrays = {"x_dram": np.ascontiguousarray(x.reshape(-1, D))}
    for name, given in _W.items():
        arrays[f"w_{name}_dram"] = np.ascontiguousarray(np.asarray(inputs[given]).T)
    for name in ("mu_r", "mu_k"):
        arrays[f"{name}_dram"] = np.ascontiguousarray(np.asarray(inputs[f"L0_ffn_{name}"]).reshape(HALVES, P).T)

    def dram(name):
        return nc.dram_tensor(name, arrays[name].shape, F32, kind="ExternalInput").ap()

    out = nc.dram_tensor("out_dram", arrays["x_dram"].shape, F32, kind="ExternalOutput").ap()
    macaron(nc, dram("x_dram"), {name: dram(f"w_{name}_dram") for name in _W},
            dram("mu_r_dram"), dram("mu_k_dram"), out)
    r = run_bass_kernel_spmd(nc, [arrays], core_ids=[0])
    return r.results[0]["out_dram"].reshape(x.shape)
```

```python
from contextlib import ExitStack

import concourse.bass as bass
from concourse import mybir

F32 = mybir.dt.float32
F32R = mybir.dt.float32r
I32 = mybir.dt.int32
ALU = mybir.AluOpType
ACT = mybir.ActivationFunctionType
AX_X = mybir.AxisListType.X

P = 128
D = 256
HALVES = D // P
HEAD = 16
TILES = 4
BLOCK = TILES * P
ROW = TILES * D
BANK = 512
LN_EPS = 1e-5
NORM_EPS = 1e-12
RSQRT_MAGIC = 0x5F3759DF
NEWTON_STEPS = 3

WEIGHTS = ("ffn_k", "ffn_r", "ffn_v", "k", "v", "u", "q")
PHASE1_FFN = ("ffn_r", "ffn_v")
PLAIN = ("ffn_r", "ffn_v", "o")


def macaron(nc, x, w_t, mu_r, mu_k, out):
    tokens = x.shape[0]
    batches, seq = 2, tokens // 2
    NB = tokens // BLOCK
    BB = seq // BLOCK
    assert x.shape[1] == D and seq % BLOCK == 0 and NB == batches * BB

    with ExitStack() as ctx:
        def sb(name, shape, dt=F32):
            return ctx.enter_context(nc.sbuf_tensor(name, shape, dt))

        def sem(name):
            return ctx.enter_context(nc.semaphore(name))

        xs = sb("xs", [P, NB * ROW])
        silu_u = sb("silu_u", [P, NB * ROW])
        q_store = sb("q_store", [P, NB * HALVES * BLOCK])
        kv_part = sb("kv_part", [P, NB * D])
        w_raw = silu_u[:, 0:len(WEIGHTS) * HALVES * D].rearrange(
            "p (n c e) -> p n c e", n=len(WEIGHTS), c=HALVES)
        split_both = [n for n in WEIGHTS if n not in PHASE1_FFN]
        w_both = [sb(f"w_{part}", [P, HALVES, len(split_both) * D], F32R) for part in ("hi", "lo")]
        mu = sb("mu", [P, 2, HALVES])
        one_mu = sb("one_mu", [P, 2, HALVES])
        ident = sb("ident", [P, P])
        head_mask = sb("head_mask", [P, P])
        keep = sb("keep", [P, 2 * NB])
        minus_half = sb("minus_half", [P, TILES])
        zeros = sb("zeros", [P, TILES])
        wait_here = sb("wait_here", [P, 4])
        stats = {k: sb("stats" + k, [P, TILES, 6]) for k in "AB"}
        meanvar = {k: sb("meanvar" + k, [P, TILES, 2]) for k in "AB"}
        var_eps = {k: sb("var_eps" + k, [P, TILES]) for k in "AB"}
        neg_mean = {k: sb("neg_mean" + k, [P, TILES]) for k in "AB"}
        rstd = {k: sb("rstd" + k, [P, TILES]) for k in "AB"}
        shift = {k: sb("shift" + k, [P, TILES]) for k in "AB"}
        kv_first = sb("kv_first", [P, D])
        kv_bd = sb("kv_bd", [P, NB * D])
        xn = {"A": sb("xnA", [P, TILES, D]),
              "B": kv_bd[:, 0:ROW].rearrange("p (t d) -> p t d", t=TILES)}
        xt = sb("xt", [P, HALVES, 1 + BLOCK])
        mix = sb("mix", [P, 2, HALVES, BLOCK])
        mix_k_hi = sb("mix_k_hi", [P, HALVES, BLOCK], F32R)
        mix_k_lo = sb("mix_k_lo", [P, HALVES, BLOCK], F32R)
        act_k = sb("act_k", [P, HALVES, BLOCK])
        gate = sb("gate", [P, 2, BANK])
        x2_hi = sb("x2_hi", [P, HALVES, BLOCK], F32R)
        x2_lo = sb("x2_lo", [P, HALVES, BLOCK], F32R)
        k_tok = kv_bd[:, ROW:2 * ROW].rearrange("p (t d) -> p t d", t=TILES)
        v_tok = sb("v_tok", [P, TILES, D])
        q_blk = sb("q_blk", [P, HALVES * BLOCK])
        heads = ROW // HEAD
        head_ss = sb("head_ss", [P, heads])
        head_rn = sb("head_rn", [P, heads])
        head_y = sb("head_y", [P, heads])
        head_t = sb("head_t", [P, heads])
        head_half = head_t[:].bitcast(I32)

        with ExitStack() as phase1_memory:
            def sb1(name, shape):
                return phase1_memory.enter_context(nc.sbuf_tensor(name, shape, F32R))

            w_ffn1 = [sb1(f"w_ffn1_{part}", [P, HALVES, len(PHASE1_FFN) * D]) for part in ("hi", "lo")]
            mix_r_hi = sb1("mix_r_hi", [P, HALVES, BLOCK])
            mix_r_lo = sb1("mix_r_lo", [P, HALVES, BLOCK])
            act_hi = sb1("act_hi", [P, HALVES, BLOCK])
            act_lo = sb1("act_lo", [P, HALVES, BLOCK])
        w_all = sb("w_plain", [P, len(PLAIN), HALVES, D])
        w_plain = {name: w_all[:, n, :, :] for n, name in enumerate(PLAIN)}
        squares = sb("squares", [P, 2, BANK])
        scale_u = sb("scale_u", [P, ROW])
        gout = sb("gout", [P, TILES, D])
        g_t = sb("g_t", [P, HALVES, BLOCK])
        mix_hi, mix_lo = (mix_k_hi, mix_r_hi), (mix_k_lo, mix_r_lo)
        w_parts = {name: (*w_both, slice(n * D, (n + 1) * D)) for n, name in enumerate(split_both)}
        w_parts |= {name: (*w_ffn1, slice(n * D, (n + 1) * D)) for n, name in enumerate(PHASE1_FFN)}

        ps01 = ctx.enter_context(nc.psum_tensor("ps01", [P, 2, BANK], F32))
        ps23 = ctx.enter_context(nc.psum_tensor("ps23", [P, 2, BANK], F32))
        ps45 = ctx.enter_context(nc.psum_tensor("ps45", [P, 2, BANK], F32))
        ps67 = ctx.enter_context(nc.psum_tensor("ps67", [P, 2, BANK], F32))

        s_x_in = sem("s_x_in")
        s_w_in = [sem(f"s_w_in_{n}") for n in WEIGHTS]
        s_mu_in = sem("s_mu_in")
        s_const = sem("s_const")
        s_plain = sem("s_plain")
        s_keep = sem("s_keep")
        s_w_hi = sem("s_w_hi")
        s_w_lo = sem("s_w_lo")
        s_bn = {k: sem("s_bn" + k) for k in "AB"}
        s_mv = {k: sem("s_mv" + k) for k in "AB"}
        s_pool = {k: sem("s_pool" + k) for k in "AB"}
        s_ln = {k: sem("s_ln" + k) for k in "AB"}
        s_xn = {k: sem("s_xn" + k) for k in "AB"}
        s_t = {k: sem("s_t" + k) for k in "AB"}
        s_halo = sem("s_halo")
        s_xt = sem("s_xt")
        s_prev = sem("s_prev")
        s_mix = sem("s_mix")
        s_mix_hi = [sem(f"s_{rk}hi") for rk in "kr"]
        s_mix_lo = [sem(f"s_{rk}lo") for rk in "kr"]
        s_k = sem("s_k")
        s_r = sem("s_r")
        s_relu_k = sem("s_relu_k")
        s_act_k = sem("s_act_k")
        s_act_hi = sem("s_act_hi")
        s_act_lo = sem("s_act_lo")
        s_gate = sem("s_gate")
        s_f = sem("s_f")
        s_gated = sem("s_gated")
        s_x1 = sem("s_x1")
        s_x2_hi = sem("s_x2_hi")
        s_x2_lo = sem("s_x2_lo")
        s_kv = sem("s_kv")
        s_kv_tok = sem("s_kv_tok")
        s_u = sem("s_u")
        s_sig_u = sem("s_sig_u")
        s_silu = sem("s_silu")
        s_q = sem("s_q")
        s_relu_q = sem("s_relu_q")
        s_kvs = sem("s_kvs")
        s_kv_part = sem("s_kv_part")
        s_sum = sem("s_sum")
        s_kv_first = sem("s_kv_first")
        s_kv_bd = sem("s_kv_bd")
        s_q_back = sem("s_q_back")
        s_o = sem("s_o")
        s_sq = sem("s_sq")
        s_ss = sem("s_ss")
        s_newton = sem("s_newton")
        s_rn = sem("s_rn")
        s_scale_u = sem("s_scale_u")
        s_gout = sem("s_gout")
        s_gt = sem("s_gt")
        s_g = sem("s_g")
        s_wo = sem("s_wo")
        s_x2 = sem("s_x2")
        s_x3 = sem("s_x3")
        s_out = sem("s_out")

        NEWTON_OPS = 3 + 3 * NEWTON_STEPS - 1

        def row(tile, block, start=0, n=ROW):
            return tile[:, bass.ds(block * ROW + start, n)]

        block = ctx.enter_context(nc.Block())

        def load_weights(eng, which):
            for n in which:
                eng.dma_start(w_raw[:, n, :, :], w_t[WEIGHTS[n]].rearrange("(c p) e -> p c e", p=P)
                              ).then_inc(s_w_in[n], 16)

        @block.sync
        def _(sp):
            def load_x(b):
                if b > 0:
                    sp.wait_ge(s_x_in, b * 16)
                sp.dma_start(row(xs, b).rearrange("p (t d) -> p t d", t=TILES),
                             x[bass.ds(b * BLOCK, BLOCK), :].rearrange("(t p) d -> p t d", p=P)
                             ).then_inc(s_x_in, 16)

            def load_q(j):
                sp.wait_ge(s_relu_q, (j + 1) * HALVES)
                if j > 0:
                    sp.wait_ge(s_o, j * 2)
                sp.dma_start(q_blk[:], row(q_store, j)).then_inc(s_q_back, 16)

            def load_plain(name):
                sp.dma_start(w_plain[name], w_t[name].rearrange("(c p) e -> p c e", p=P)).then_inc(s_plain, 16)

            def store_x(b):
                sp.wait_ge(s_x3, (b + 1) * 2)
                sp.dma_start(out[bass.ds(b * BLOCK, BLOCK), :].rearrange("(t p) d -> p t d", p=P),
                             row(xs, b).rearrange("p (t d) -> p t d", t=TILES)).then_inc(s_out, 16)

            load_x(0)
            load_weights(sp, range(2, len(WEIGHTS)))
            for b in range(1, NB):
                load_x(b)
            load_q(0)
            sp.wait_ge(s_f, 2 * NB)
            for name in PLAIN:
                load_plain(name)
            for j in range(1, 3):
                load_q(j)
            for j in range(3, NB):
                load_q(j)
                store_x(j - 3)
            for b in range(NB - 3, NB):
                store_x(b)
            sp.wait_ge(s_out, 16 * NB)

        @block.gpsimd
        def _(pool):
            nc.gpsimd.memset(ident[:], 0.0).then_inc(s_const, 1)
            nc.gpsimd.memset(head_mask[:], 1.0 / HEAD).then_inc(s_const, 1)
            nc.gpsimd.memset(minus_half[:], -0.5).then_inc(s_const, 1)
            nc.gpsimd.memset(zeros[:], 0.0).then_inc(s_const, 1)
            pool.wait_ge(s_const, 4)
            nc.gpsimd.affine_select(out=ident[:], in_=ident[:], compare_op=ALU.not_equal, fill=1.0, base=0,
                                    pattern=[[-1, P]], channel_multiplier=1).then_inc(s_const, 1)
            by_head = head_mask[:].rearrange("p (h e) -> p h e", e=HEAD)
            nc.gpsimd.affine_select(out=by_head, in_=by_head, compare_op=ALU.is_ge, fill=0.0, base=0,
                                    pattern=[[-HEAD, P // HEAD], [0, HEAD]],
                                    channel_multiplier=1).then_inc(s_const, 1)
            pool.wait_ge(s_const, 6)
            nc.gpsimd.affine_select(out=by_head, in_=by_head, compare_op=ALU.is_ge, fill=0.0, base=HEAD - 1,
                                    pattern=[[HEAD, P // HEAD], [0, HEAD]],
                                    channel_multiplier=-1).then_inc(s_const, 1)

            def ln_scales(kind, n, first=False):
                pool.wait_ge(s_mv[kind], (n + 1) * TILES)
                nc.gpsimd.tensor_tensor(neg_mean[kind][:], zeros[:], meanvar[kind][:, :, 0],
                                        ALU.subtract).then_inc(s_pool[kind], 1)
                nc.gpsimd.tensor_scalar(var_eps[kind][:], meanvar[kind][:, :, 1], 1.0, LN_EPS,
                                        ALU.mult, ALU.add).then_inc(s_pool[kind], 1)
                pool.wait_ge(s_pool[kind], (n + 1) * 2)
                if not first:
                    pool.wait_ge(s_xn[kind], n * TILES)
                nc.gpsimd.tensor_tensor(rstd[kind][:], var_eps[kind][:], minus_half[:],
                                        ALU.pow).then_inc(s_ln[kind], 1)
                pool.wait_ge(s_ln[kind], n * 2 + 1)
                nc.gpsimd.tensor_tensor(shift[kind][:], neg_mean[kind][:], rstd[kind][:],
                                        ALU.mult).then_inc(s_ln[kind], 1)

            def mix_low(rk, f, first=False):
                for h in range(HALVES):
                    pool.wait_ge(s_mix_hi[rk], f * 2 + h + 1)
                    if not first and h == 0:
                        pool.wait_ge((s_k, s_r)[rk], f * 2)
                    nc.gpsimd.tensor_tensor(mix_lo[rk][:, h, :], mix[:, rk, h, :],
                                            mix_hi[rk][:, h, :].bitcast(F32),
                                            ALU.subtract).then_inc(s_mix_lo[rk], 1)

            def square_k(f):
                for h in range(HALVES):
                    pool.wait_ge(s_act_hi, f * 2 + h + 1)
                    nc.gpsimd.tensor_tensor(act_k[:, h, :], act_k[:, h, :], act_k[:, h, :],
                                            ALU.mult).then_inc(s_act_k, 1)

            def act_low(f, first=False):
                for h in range(HALVES):
                    pool.wait_ge(s_act_k, f * 2 + h + 1)
                    if not first and h == 0:
                        pool.wait_ge(s_f, f * 2)
                    nc.gpsimd.tensor_tensor(act_lo[:, h, :], act_k[:, h, :],
                                            act_hi[:, h, :].bitcast(F32), ALU.subtract).then_inc(s_act_lo, 1)

            def scale_gate(j, first=False):
                pool.wait_ge(s_rn, j + 1)
                if not first:
                    pool.wait_ge(s_gout, j * 2)
                nc.gpsimd.tensor_tensor(scale_u[:].rearrange("p (n e) -> p n e", e=HEAD),
                                        row(silu_u, j).rearrange("p (n e) -> p n e", e=HEAD),
                                        head_rn[:].unsqueeze(2).to_broadcast([P, heads, HEAD]),
                                        ALU.mult).then_inc(s_scale_u, 1)

            def add_ffn2(f):
                b = f - NB
                for n in range(2):
                    pool.wait_ge(s_gated, f * 2 + n + 1)
                    xb = row(xs, b, n * BANK, BANK)
                    nc.gpsimd.tensor_tensor(xb, xb, gate[:, n, :], ALU.add).then_inc(s_x3, 1)

            ln_scales("A", 0, first=True)
            mix_low(0, 0, first=True)
            ln_scales("A", 1)
            mix_low(1, 0, first=True)
            square_k(0)
            act_low(0, first=True)
            mix_low(0, 1)
            ln_scales("B", 0, first=True)
            mix_low(1, 1)
            with pool.Fori(1, NB - 1) as i:
                square_k(i)
                ln_scales("A", i + 1)
                act_low(i)
                mix_low(0, i + 1)
                ln_scales("B", i)
                mix_low(1, i + 1)
            square_k(NB - 1)
            act_low(NB - 1)
            ln_scales("B", NB - 1)
            scale_gate(0, first=True)
            ln_scales("A", NB)
            scale_gate(1)
            mix_low(0, NB)
            with pool.Fori(2, NB) as j:
                scale_gate(j)
                ln_scales("A", j + (NB - 1))
                add_ffn2(j + (NB - 2))
                mix_low(0, j + (NB - 1))
            ln_scales("A", 2 * NB - 1)
            add_ffn2(2 * NB - 2)
            mix_low(0, 2 * NB - 1)
            add_ffn2(2 * NB - 1)

        @block.scalar
        def _(act):
            load_weights(act, range(2))
            act.dma_start(mu[:, 0, :], mu_k).then_inc(s_mu_in, 16)
            act.dma_start(mu[:, 1, :], mu_r).then_inc(s_mu_in, 16)

            def split_weights(lo, hi):
                for n in range(lo, hi):
                    act.wait_ge(s_w_in[n], 16)
                    w_hi, _, cols = w_parts[WEIGHTS[n]]
                    nc.scalar.activation(w_hi[:, :, cols], w_raw[:, n, :, :], ACT.Identity,
                                         scale=0.5 if WEIGHTS[n] == "ffn_v" else 1.0).then_inc(s_w_hi, 1)

            def normalize(kind, n, b, first=False):
                act.wait_ge(s_ln[kind], (n + 1) * 2)
                if not first:
                    act.wait_ge(s_t[kind], n * HALVES)
                for t in range(TILES):
                    nc.scalar.activation(xn[kind][:, t, :], row(xs, b, t * D, D), ACT.Identity,
                                         bias=shift[kind][:, t:t + 1],
                                         scale=rstd[kind][:, t:t + 1]).then_inc(s_xn[kind], 1)

            def previous(f, rk, h):
                act.wait_ge(s_xt, f * 2 + h + 1)
                nc.scalar.activation(mix[:, rk, h, :], xt[:, h, 0:BLOCK], ACT.Copy,
                                     scale=one_mu[:, rk, h:h + 1]).then_inc(s_prev, 1)

            def previous_k(f, first=False):
                if first:
                    act.wait_ge(s_keep, 4)
                else:
                    act.wait_ge(s_mix, f * 4)
                    nc.scalar.activation(xt[:, :, 0:1], xt[:, :, BLOCK:BLOCK + 1], ACT.Copy,
                                         scale=keep[:, bass.ds(f, 1)]).then_inc(s_halo, 1)
                    act.wait_ge(s_halo, f * 1)
                    act.wait_ge(s_mix_lo[0], f * 2)
                for h in range(HALVES):
                    act.wait_ge(s_t["A"], f * 2 + h + 1)
                    nc.scalar.activation(xt[:, h, 1:1 + BLOCK], ps23[:, h, :], ACT.Identity).then_inc(s_xt, 1)
                    previous(f, 0, h)

            def previous_r(f, s_used=None):
                if s_used is not None:
                    act.wait_ge(s_used, f * 2)
                for h in range(HALVES):
                    previous(f, 1, h)

            def mix_high(f, rk, first=False):
                if not first:
                    act.wait_ge((s_k, s_r)[rk], f * 2)
                for h in range(HALVES):
                    act.wait_ge(s_mix, f * 4 + rk * 2 + h + 1)
                    nc.scalar.activation(mix_hi[rk][:, h, :], mix[:, rk, h, :],
                                         ACT.Identity).then_inc(s_mix_hi[rk], 1)

            def relu_k(f, h):
                act.wait_ge(s_k, f * 2 + h + 1)
                nc.scalar.activation(act_k[:, h, :], ps23[:, h, :], ACT.Relu).then_inc(s_relu_k, 1)

            def square_high(f, h):
                act.wait_ge(s_relu_k, f * 2 + h + 1)
                nc.scalar.activation(act_hi[:, h, :], act_k[:, h, :], ACT.Square).then_inc(s_act_hi, 1)

            def activate_k(f, first=False):
                if not first:
                    act.wait_ge(s_act_lo, f * 2)
                relu_k(f, 0)
                if not first:
                    act.wait_ge(s_f, f * 2)
                square_high(f, 0)
                relu_k(f, 1)
                square_high(f, 1)

            def activate_k_plain(f):
                act.wait_ge(s_f, f * 2)
                for h in range(HALVES):
                    relu_k(f, h)
                    act.wait_ge(s_relu_k, f * 2 + h + 1)
                    nc.scalar.activation(act_k[:, h, :], act_k[:, h, :], ACT.Square).then_inc(s_act_k, 1)

            def sigmoid_r(f, s_added=None, added=0):
                for n in range(2):
                    act.wait_ge(s_r, f * 2 + n + 1)
                    if s_added is not None and n == 0:
                        act.wait_ge(s_added, added)
                    nc.scalar.activation(gate[:, n, :], ps45[:, n, :], ACT.Sigmoid).then_inc(s_gate, 1)

            def x2_high(a, ps=ps01, first=False):
                for h in range(HALVES):
                    act.wait_ge(s_t["B"], a * 2 + h + 1)
                    if not first and h == 0:
                        act.wait_ge(s_q, a * 2)
                    nc.scalar.activation(x2_hi[:, h, :], ps[:, h, :], ACT.Identity).then_inc(s_x2_hi, 1)

            def sigmoid_u(a, first=False):
                for n in range(2):
                    act.wait_ge(s_u, a * 2 + n + 1)
                    if first and n == 0:
                        act.wait_ge(s_w_lo, len(WEIGHTS))
                    nc.scalar.activation(row(silu_u, a, n * BANK, BANK), ps01[:, n, :], ACT.Sigmoid).then_inc(s_sig_u, 1)

            def relu_q(a):
                for h in range(HALVES):
                    act.wait_ge(s_q, a * 2 + h + 1)
                    nc.scalar.activation(row(q_store, a, h * BLOCK, BLOCK), ps67[:, h, :],
                                         ACT.Relu).then_inc(s_relu_q, 1)

            def square_heads(j, ps=ps67, first=False):
                for n in range(2):
                    act.wait_ge(s_o, j * 2 + n + 1)
                    if not first and n == 0:
                        act.wait_ge(s_ss, j * 2)
                    nc.scalar.activation(squares[:, n, :], ps[:, n, :], ACT.Square,
                                         scale=float(HEAD) ** -0.5).then_inc(s_sq, 1)

            def copy_g(j, ps=ps67, first=False):
                for h in range(HALVES):
                    act.wait_ge(s_gt, j * 2 + h + 1)
                    if not first and h == 0:
                        act.wait_ge(s_wo, j * 2)
                    nc.scalar.activation(g_t[:, h, :], ps[:, h, :], ACT.Identity).then_inc(s_g, 1)

            split_weights(0, 2)
            normalize("A", 0, 0, first=True)
            previous_k(0, first=True)
            previous_r(0)
            mix_high(0, 0, first=True)
            mix_high(0, 1, first=True)
            normalize("A", 1, 1)
            split_weights(2, 3)
            activate_k(0, first=True)
            sigmoid_r(0)
            previous_k(1)
            previous_r(1, s_mix_lo[1])
            mix_high(1, 0)
            mix_high(1, 1)
            split_weights(3, len(WEIGHTS))

            def phase1(i, first=False):
                normalize("B", i - 1, i - 1, first=first)
                activate_k(i)
                x2_high(i - 1, first=first)
                sigmoid_r(i, s_x1, i * 2)
                normalize("A", i + 1, i + 1)
                previous_k(i + 1)
                previous_r(i + 1, s_mix_lo[1])
                mix_high(i + 1, 0)
                sigmoid_u(i - 1, first=first)
                mix_high(i + 1, 1)
                relu_q(i - 1)

            phase1(1, first=True)
            with act.Fori(2, NB - 1) as i:
                phase1(i)
            normalize("B", NB - 2, NB - 2)
            activate_k(NB - 1)
            x2_high(NB - 2)
            sigmoid_r(NB - 1, s_x1, 2 * (NB - 1))
            square_heads(0, ps23, first=True)
            sigmoid_u(NB - 2)
            relu_q(NB - 2)
            normalize("B", NB - 1, NB - 1)
            x2_high(NB - 1, ps45)
            copy_g(0, ps23, first=True)
            sigmoid_u(NB - 1)
            square_heads(1, ps23)
            relu_q(NB - 1)
            normalize("A", NB, 0)
            copy_g(1)
            previous_k(NB)
            mix_high(NB, 0)
            square_heads(2)
            previous_r(NB, s_r)

            def phase2(j, s_added, added, last=False):
                activate_k_plain(j + (NB - 2))
                sigmoid_r(j + (NB - 2), s_added, added)
                normalize("A", j + (NB - 1), j - 1)
                copy_g(j)
                previous_k(j + (NB - 1))
                mix_high(j + (NB - 1), 0)
                if not last:
                    square_heads(j + 1)
                previous_r(j + (NB - 1), s_r)

            phase2(2, s_x1, 2 * NB)
            with act.Fori(3, NB - 1) as j:
                phase2(j, s_x3, (j - 2) * 2)
            phase2(NB - 1, s_x3, 2 * (NB - 3), last=True)
            activate_k_plain(2 * NB - 2)
            sigmoid_r(2 * NB - 2, s_x3, 2 * (NB - 2))
            normalize("A", 2 * NB - 1, NB - 1)
            previous_k(2 * NB - 1)
            mix_high(2 * NB - 1, 0)
            previous_r(2 * NB - 1, s_r)
            activate_k_plain(2 * NB - 1)
            sigmoid_r(2 * NB - 1, s_x3, 2 * (NB - 1))

        @block.vector
        def _(dve):
            nc.vector.memset(keep[:], 1.0).then_inc(s_keep, 1)
            nc.vector.memset(xt[:, :, 0:1], 0.0).then_inc(s_keep, 1)
            dve.wait_ge(s_keep, 2)
            nc.vector.memset(keep[:, 0:2 * NB:BB], 0.0).then_inc(s_keep, 1)
            dve.wait_ge(s_mu_in, 32)
            nc.vector.tensor_scalar(one_mu[:], mu[:], -1.0, 1.0, ALU.mult, ALU.add).then_inc(s_keep, 1)

            def split_weights(lo, hi):
                for n in range(lo, hi):
                    dve.wait_ge(s_w_hi, n + 1)
                    w_hi, w_lo, cols = w_parts[WEIGHTS[n]]
                    nc.vector.scalar_tensor_tensor(
                        out=w_lo[:, :, cols], in0=w_raw[:, n, :, :],
                        scalar=0.5 if WEIGHTS[n] == "ffn_v" else 1.0,
                        in1=w_hi[:, :, cols].bitcast(F32), op0=ALU.mult, op1=ALU.subtract).then_inc(s_w_lo, 1)

            def ln_stats(kind, n, b, first=False):
                col = 2 * "AB".index(kind)
                if not first:
                    dve.wait_ge(s_mv[kind], n * TILES)
                nc.vector.memset(wait_here[:, col:col + 1], 0.0)
                for t in range(TILES):
                    nc.vector.bn_stats(stats[kind][:, t, :], row(xs, b, t * D, D)).then_inc(s_bn[kind], 1)
                if not first:
                    dve.wait_ge(s_ln[kind], n * 2)
                dve.wait_ge(s_bn[kind], (n + 1) * TILES)
                nc.vector.memset(wait_here[:, col + 1:col + 2], 0.0)
                for t in range(TILES):
                    nc.vector.bn_aggr(meanvar[kind][:, t, :], stats[kind][:, t, :]).then_inc(s_mv[kind], 1)

            def mix_current(rk, f):
                for h in range(HALVES):
                    dve.wait_ge(s_prev, f * 4 + rk * 2 + h + 1)
                    m = mix[:, rk, h, :]
                    nc.vector.scalar_tensor_tensor(out=m, in0=xt[:, h, 1:1 + BLOCK], scalar=mu[:, rk, h:h + 1],
                                                   in1=m, op0=ALU.mult, op1=ALU.add).then_inc(s_mix, 1)

            def gate_ffn(f, half=False):
                for n in range(2):
                    dve.wait_ge(s_f, f * 2 + n + 1)
                    dve.wait_ge(s_gate, f * 2 + n + 1)
                    if half:
                        gated = nc.vector.scalar_tensor_tensor(out=gate[:, n, :], in0=ps45[:, n, :], scalar=0.5,
                                                               in1=gate[:, n, :], op0=ALU.mult, op1=ALU.mult)
                    else:
                        gated = nc.vector.tensor_tensor(gate[:, n, :], ps45[:, n, :], gate[:, n, :], ALU.mult)
                    gated.then_inc(s_gated, 1)

            def add_ffn1(f):
                for n in range(2):
                    dve.wait_ge(s_gated, f * 2 + n + 1)
                    xb = row(xs, f, n * BANK, BANK)
                    nc.vector.tensor_tensor(xb, xb, gate[:, n, :], ALU.add).then_inc(s_x1, 1)

            def x2_low(a, ps=ps01):
                for h in range(HALVES):
                    dve.wait_ge(s_x2_hi, a * 2 + h + 1)
                    nc.vector.tensor_tensor(x2_lo[:, h, :], ps[:, h, :], x2_hi[:, h, :].bitcast(F32),
                                            ALU.subtract).then_inc(s_x2_lo, 1)

            def keep_kv(a, first=False):
                for t in range(TILES):
                    dve.wait_ge(s_kv, a * TILES + t + 1)
                    if not first and t == 0:
                        dve.wait_ge(s_kvs, a * 1)
                    nc.vector.tensor_copy(v_tok[:, t, :], ps67[:, t % 2, D:2 * D]).then_inc(s_kv_tok, 1)
                    nc.vector.tensor_scalar(k_tok[:, t, :], ps67[:, t % 2, 0:D], 0.0, None,
                                            ALU.max).then_inc(s_kv_tok, 1)

            def silu(a, n):
                dve.wait_ge(s_sig_u, a * 2 + n + 1)
                su = row(silu_u, a, n * BANK, BANK)
                nc.vector.tensor_tensor(su, ps01[:, n, :], su, ALU.mult).then_inc(s_silu, 1)

            def keep_kv_part(a):
                dve.wait_ge(s_kvs, a + 1)
                nc.vector.tensor_copy(kv_part[:, bass.ds(a * D, D)], ps01[:, 0, 0:D]).then_inc(s_kv_part, 1)

            def sum_kv(batch):
                first = batch * BB
                part = [kv_part[:, (first + n) * D:(first + n + 1) * D] for n in range(BB)]
                dve.wait_ge(s_kv_part, first + BB)
                for n in range(1, BB):
                    if n > 1:
                        dve.wait_ge(s_sum, batch * (BB - 1) + n - 1)
                    nc.vector.tensor_tensor(part[0], part[0], part[n], ALU.add).then_inc(s_sum, 1)

            def diagonal_kv(batch, dst):
                return nc.vector.tensor_tensor(
                    dst.rearrange("p (h e) -> p h e", h=HALVES),
                    kv_part[:, batch * BB * D:(batch * BB + 1) * D].rearrange("p (h e) -> p h e", h=HALVES),
                    head_mask[:].unsqueeze(1).to_broadcast([P, HALVES, P]), ALU.mult)

            def keep_kv_of_first():
                dve.wait_ge(s_sum, BB - 1)
                dve.wait_ge(s_const, 7)
                diagonal_kv(0, kv_first[:]).then_inc(s_kv_first, 1)

            def place_kv(batch):
                dve.wait_ge(s_sum, (batch + 1) * (BB - 1))
                if batch == 0:
                    dve.wait_ge(s_t["B"], 2 * NB)
                    dve.wait_ge(s_kvs, NB)
                for n in range(BB):
                    first = (batch * BB + n) * D
                    diagonal_kv(batch, kv_bd[:, first:first + D]).then_inc(s_kv_bd, 1)

            def add_attention(j, n, ps=ps01):
                dve.wait_ge(s_wo, j * 2 + n + 1)
                xb = row(xs, j, n * BANK, BANK)
                nc.vector.tensor_tensor(xb, xb, ps[:, n, :], ALU.add).then_inc(s_x2, 1)

            def head_norms(j, attention_of=None, mix_of=None, first=False):
                for n in range(2):
                    dve.wait_ge(s_sq, j * 2 + n + 1)
                    nc.vector.tensor_reduce(head_ss[:, n * heads // 2:(n + 1) * heads // 2],
                                            squares[:, n, :].rearrange("p (g e) -> p g e", e=HEAD),
                                            AX_X, ALU.add).then_inc(s_ss, 1)
                if mix_of is not None:
                    mix_current(1, mix_of)
                dve.wait_ge(s_ss, (j + 1) * 2)
                step = [0]

                def then(ins, meanwhile=None):
                    step[0] += 1
                    ins.then_inc(s_newton, 1)
                    if meanwhile is not None:
                        meanwhile()
                    dve.wait_ge(s_newton, j * NEWTON_OPS + step[0])

                then(nc.vector.tensor_scalar(head_ss[:], head_ss[:], NORM_EPS ** 2, None, ALU.max))
                then(nc.vector.tensor_scalar(head_half, head_ss[:].bitcast(I32), 1, None,
                                             ALU.arith_shift_right))
                then(nc.vector.tensor_scalar(head_y[:].bitcast(I32), head_half, -1.0, float(RSQRT_MAGIC),
                                             ALU.mult, ALU.add))
                if not first:
                    dve.wait_ge(s_scale_u, j * 1)
                for n in range(NEWTON_STEPS):
                    last = n == NEWTON_STEPS - 1
                    then(nc.vector.tensor_tensor(head_t[:], head_y[:], head_y[:], ALU.mult))
                    then(nc.vector.scalar_tensor_tensor(out=head_t[:], in0=head_t[:], scalar=-0.5,
                                                        in1=head_ss[:], op0=ALU.mult, op1=ALU.mult))
                    y = nc.vector.scalar_tensor_tensor(out=head_rn[:] if last else head_y[:], in0=head_t[:],
                                                       scalar=1.5, in1=head_y[:], op0=ALU.add, op1=ALU.mult)
                    if last:
                        y.then_inc(s_rn, 1)
                    elif not first and attention_of is not None:
                        then(y, lambda: add_attention(attention_of, n))
                    else:
                        then(y)
                assert step[0] == NEWTON_OPS

            def gate_heads(j, ps=ps67, first=False):
                dve.wait_ge(s_scale_u, j + 1)
                if not first:
                    dve.wait_ge(s_gt, j * 2)
                for n in range(2):
                    nc.vector.tensor_tensor(gout[:, 2 * n:2 * n + 2, :],
                                            ps[:, n, :].rearrange("p (t d) -> p t d", t=2),
                                            scale_u[:, n * BANK:(n + 1) * BANK].rearrange("p (t d) -> p t d", t=2),
                                            ALU.mult).then_inc(s_gout, 1)

            def stats_of_input(f, first=False):
                dve.wait_ge(s_x_in, (f + 1) * 16)
                ln_stats("A", f, f, first=first)

            def stats_of_x1(a, first=False):
                dve.wait_ge(s_x1, (a + 1) * 2)
                ln_stats("B", a, a, first=first)

            def stats_of_x2(f, b):
                dve.wait_ge(s_x2, (b + 1) * 2)
                ln_stats("A", f, b)

            stats_of_input(0, first=True)
            split_weights(0, 2)
            stats_of_input(1)
            mix_current(0, 0)
            mix_current(1, 0)
            split_weights(2, 3)
            mix_current(0, 1)
            gate_ffn(0)
            add_ffn1(0)
            mix_current(1, 1)
            stats_of_x1(0, first=True)
            split_weights(3, len(WEIGHTS))

            def phase1(i, first=False):
                stats_of_input(i + 1)
                x2_low(i - 1)
                keep_kv(i - 1, first=first)
                mix_current(0, i + 1)
                gate_ffn(i)
                add_ffn1(i)
                silu(i - 1, 0)
                stats_of_x1(i)
                silu(i - 1, 1)
                mix_current(1, i + 1)
                keep_kv_part(i - 1)

            phase1(1, first=True)
            with dve.Fori(2, NB - 1) as i:
                phase1(i)
            sum_kv(0)
            keep_kv_of_first()
            x2_low(NB - 2)
            keep_kv(NB - 2)
            gate_ffn(NB - 1)
            add_ffn1(NB - 1)
            silu(NB - 2, 0)
            stats_of_x1(NB - 1)
            silu(NB - 2, 1)
            head_norms(0, first=True)
            keep_kv_part(NB - 2)
            x2_low(NB - 1, ps45)
            gate_heads(0, ps23, first=True)
            keep_kv(NB - 1)
            silu(NB - 1, 0)
            silu(NB - 1, 1)
            add_attention(0, 0, ps45)
            add_attention(0, 1, ps45)
            stats_of_x2(NB, 0)
            head_norms(1)
            keep_kv_part(NB - 1)
            gate_heads(1, ps23)
            place_kv(0)
            sum_kv(1)
            place_kv(1)
            mix_current(0, NB)

            with dve.Fori(2, NB) as j:
                head_norms(j, attention_of=j - 1, mix_of=j + (NB - 2))
                stats_of_x2(j + (NB - 1), j - 1)
                gate_heads(j)
                gate_ffn(j + (NB - 2), half=True)
                mix_current(0, j + (NB - 1))
            mix_current(1, 2 * NB - 2)
            for n in range(2):
                add_attention(NB - 1, n)
            stats_of_x2(2 * NB - 1, NB - 1)
            gate_ffn(2 * NB - 2, half=True)
            mix_current(0, 2 * NB - 1)
            mix_current(1, 2 * NB - 1)
            gate_ffn(2 * NB - 1, half=True)

        @block.tensor
        def _(pe):
            def product(dst, a_hi, a_lo, b_hi, b_lo, start, stop):
                nc.tensor.matmul(dst, a_hi, b_hi, start=start, stop=False)
                nc.tensor.matmul(dst, a_hi, b_lo, start=False, stop=False)
                return nc.tensor.matmul(dst, a_lo, b_hi, start=False, stop=stop)

            def weight(name, c, start=0, n=D):
                w_hi, w_lo, cols = w_parts[name]
                cols = slice(cols.start + start, cols.start + start + n)
                return w_hi[:, c, cols], w_lo[:, c, cols]

            def token_rows(hi, lo, c, t):
                cols = slice(t * P, (t + 1) * P)
                return hi[:, c, cols], lo[:, c, cols]

            def to_features(kind, n, ps):
                for h in range(HALVES):
                    for t in range(TILES):
                        if h == 0:
                            pe.wait_ge(s_xn[kind], n * TILES + t + 1)
                        last = nc.tensor.transpose(ps[:, h, t * P:(t + 1) * P],
                                                   xn[kind][:, t, h * P:(h + 1) * P], ident[:])
                    last.then_inc(s_t[kind], 1)

            def transpose_a(f, first=False):
                if not first:
                    pe.wait_ge(s_relu_k, f * 2)
                to_features("A", f, ps23)

            def ffn_k(f):
                for m in range(HALVES):
                    for c in range(HALVES):
                        if m == 0:
                            pe.wait_ge(s_mix_hi[0], f * 2 + c + 1)
                            pe.wait_ge(s_mix_lo[0], f * 2 + c + 1)
                        last = product(ps23[:, m, :], *weight("ffn_k", c, m * P, P),
                                       mix_hi[0][:, c, :], mix_lo[0][:, c, :], c == 0, c == HALVES - 1)
                    last.then_inc(s_k, 1)

            def by_tiles(ps, hi, lo, name, s_done, s_free=None, free=0, tiles=range(TILES)):
                for t in tiles:
                    if t % 2 == 0 and s_free is not None:
                        pe.wait_ge(s_free, free + t // 2)
                    for c in range(HALVES):
                        last = product(ps[:, t // 2, (t % 2) * D:(t % 2 + 1) * D], *token_rows(hi, lo, c, t),
                                       *weight(name, c), c == 0, c == HALVES - 1)
                    if t % 2:
                        last.then_inc(s_done, 1)

            def by_tiles_plain(ps, operand, name, s_done, s_free=None, free=0):
                for t in range(TILES):
                    if t % 2 == 0 and s_free is not None:
                        pe.wait_ge(s_free, free + t // 2)
                    for c in range(HALVES):
                        last = nc.tensor.matmul(ps[:, t // 2, (t % 2) * D:(t % 2 + 1) * D],
                                                operand[:, c, t * P:(t + 1) * P], w_plain[name][:, c, :],
                                                start=(c == 0), stop=(c == HALVES - 1))
                    if t % 2:
                        last.then_inc(s_done, 1)

            def ffn_r_plain(f):
                pe.wait_ge(s_mix, f * 4 + 4)
                pe.wait_ge(s_gated, f * 2)
                by_tiles_plain(ps45, mix[:, 1, :, :], "ffn_r", s_r)

            def ffn_v_plain(f):
                pe.wait_ge(s_act_k, f * 2 + 2)
                by_tiles_plain(ps45, act_k, "ffn_v", s_f, s_gate, f * 2 + 1)

            def ffn_r(f, first=False, tiles=range(TILES)):
                if 0 in tiles:
                    pe.wait_ge(s_mix_hi[1], f * 2 + 2)
                    pe.wait_ge(s_mix_lo[1], f * 2 + 2)
                    if not first:
                        pe.wait_ge(s_gated, f * 2)
                by_tiles(ps45, mix_hi[1], mix_lo[1], "ffn_r", s_r, tiles=tiles)

            def ffn_v(f):
                pe.wait_ge(s_act_hi, f * 2 + 2)
                pe.wait_ge(s_act_lo, f * 2 + 2)
                by_tiles(ps45, act_hi, act_lo, "ffn_v", s_f, s_gate, f * 2 + 1)

            def wait_ps01(a):
                pe.wait_ge(s_kv_part, a * 1)
                pe.wait_ge(s_silu, a * 2)

            def transpose_b(a, first=False):
                if not first:
                    wait_ps01(a)
                to_features("B", a, ps01)

            def kv_of_tokens(a, first=False):
                pe.wait_ge(s_x2_hi, a * 2 + 2)
                pe.wait_ge(s_x2_lo, a * 2 + 2)
                if not first:
                    pe.wait_ge(s_relu_q, a * 2)
                for t in range(TILES):
                    if t >= 2:
                        pe.wait_ge(s_kv_tok, a * 8 + 2 * (t - 1))
                    for c in range(HALVES):
                        last = product(ps67[:, t % 2, :], *token_rows(x2_hi, x2_lo, c, t),
                                       *weight("k", c, 0, 2 * D), c == 0, c == HALVES - 1)
                    last.then_inc(s_kv, 1)

            def u_of_tokens(a):
                by_tiles(ps01, x2_hi, x2_lo, "u", s_u)

            def q_of_tokens(a):
                pe.wait_ge(s_kv_tok, a * 8 + 8)
                for m in range(HALVES):
                    for c in range(HALVES):
                        last = product(ps67[:, m, :], *weight("q", c, m * P, P),
                                       x2_hi[:, c, :], x2_lo[:, c, :], c == 0, c == HALVES - 1)
                    last.then_inc(s_q, 1)

            def sum_kv_of_block(a):
                pe.wait_ge(s_kv_tok, a * 8 + 8)
                pe.wait_ge(s_silu, a * 2 + 1)
                for h in range(HALVES):
                    half = slice(h * P, (h + 1) * P)
                    for t in range(TILES):
                        last = nc.tensor.matmul(ps01[:, 0, half], k_tok[:, t, half], v_tok[:, t, half],
                                                start=(t == 0), stop=(t == TILES - 1))
                last.then_inc(s_kvs, 1)

            def attend(j, ps, kv, at):
                pe.wait_ge(s_q_back, (j + 1) * 16)
                for t in range(TILES):
                    for h in range(HALVES):
                        last = nc.tensor.matmul(
                            ps[:, t // 2, (t % 2) * D + h * P:(t % 2) * D + (h + 1) * P],
                            q_blk[:, h * BLOCK + t * P:h * BLOCK + (t + 1) * P],
                            kv[:, bass.ds(at + h * P, P)], start=True, stop=True)
                    if t % 2:
                        last.then_inc(s_o, 1)

            def transpose_g(j, ps=ps67):
                pe.wait_ge(s_gout, j * 2 + 2)
                for h in range(HALVES):
                    for t in range(TILES):
                        last = nc.tensor.transpose(ps[:, h, t * P:(t + 1) * P],
                                                   gout[:, t, h * P:(h + 1) * P], ident[:])
                    last.then_inc(s_gt, 1)

            def project_out(j, ps=ps01):
                pe.wait_ge(s_g, j * 2 + 2)
                by_tiles_plain(ps, g_t, "o", s_wo)

            pe.wait_ge(s_const, 7)
            transpose_a(0, first=True)
            pe.wait_ge(s_w_lo, 2)
            ffn_k(0)
            ffn_r(0, first=True)
            transpose_a(1)
            pe.wait_ge(s_w_lo, 3)
            ffn_v(0)

            def phase1(i, first=False):
                ffn_k(i)
                ffn_r(i, tiles=(0, 1))
                transpose_b(i - 1, first=first)
                ffn_r(i, tiles=(2, 3))
                if first:
                    pe.wait_ge(s_w_lo, len(WEIGHTS))
                kv_of_tokens(i - 1, first=first)
                transpose_a(i + 1)
                ffn_v(i)
                u_of_tokens(i - 1)
                q_of_tokens(i - 1)
                sum_kv_of_block(i - 1)

            phase1(1, first=True)
            with pe.Fori(2, NB - 1) as i:
                phase1(i)
            ffn_k(NB - 1)
            ffn_r(NB - 1, tiles=(0, 1))
            transpose_b(NB - 2)
            ffn_r(NB - 1, tiles=(2, 3))
            kv_of_tokens(NB - 2)
            ffn_v(NB - 1)
            pe.wait_ge(s_kv_first, 1)
            pe.wait_ge(s_relu_k, 2 * NB)
            attend(0, ps23, kv_first, 0)
            u_of_tokens(NB - 2)
            q_of_tokens(NB - 2)
            pe.wait_ge(s_gated, 2 * NB)
            to_features("B", NB - 1, ps45)
            sum_kv_of_block(NB - 2)
            kv_of_tokens(NB - 1)
            transpose_g(0, ps23)
            wait_ps01(NB - 1)
            u_of_tokens(NB - 1)
            pe.wait_ge(s_plain, 16 * len(PLAIN))
            project_out(0, ps45)
            attend(1, ps23, kv_first, 0)
            q_of_tokens(NB - 1)
            sum_kv_of_block(NB - 1)
            pe.wait_ge(s_relu_q, 2 * NB)
            transpose_g(1)
            transpose_a(NB)
            wait_ps01(NB)
            pe.wait_ge(s_kv_bd, NB)
            with pe.Fori(2, NB) as j:
                pe.wait_ge(s_g, j * 2)
                attend(j, ps67, kv_bd, j * D)
                pe.wait_ge(s_x2, (j - 1) * 2)
                project_out(j - 1)
                ffn_k(j + (NB - 2))
                ffn_r_plain(j + (NB - 2))
                ffn_v_plain(j + (NB - 2))
                transpose_g(j)
                transpose_a(j + (NB - 1))
            pe.wait_ge(s_x2, (NB - 1) * 2)
            project_out(NB - 1)
            ffn_k(2 * NB - 2)
            ffn_r_plain(2 * NB - 2)
            ffn_v_plain(2 * NB - 2)
            transpose_a(2 * NB - 1)
            ffn_k(2 * NB - 1)
            ffn_r_plain(2 * NB - 1)
            ffn_v_plain(2 * NB - 1)


_W = {"ffn_k": "L0_ffn_W_k", "ffn_r": "L0_ffn_W_r", "ffn_v": "L0_ffn_W_v", "k": "L0_attn_Wk",
      "v": "L0_attn_Wv", "u": "L0_attn_Wu", "q": "L0_attn_Wq", "o": "L0_attn_Wo"}


def kernel(**inputs):
    import numpy as np
    import concourse.bacc as bacc
    from concourse.bass_utils import run_bass_kernel_spmd

    nc = bacc.Bacc("TRN2", target_bir_lowering=False, num_devices=1)
    x = np.asarray(inputs["L0_attn_x"])
    arrays = {"x_dram": np.ascontiguousarray(x.reshape(-1, D))}
    for name, given in _W.items():
        arrays[f"w_{name}_dram"] = np.ascontiguousarray(np.asarray(inputs[given]).T)
    for name in ("mu_r", "mu_k"):
        arrays[f"{name}_dram"] = np.ascontiguousarray(np.asarray(inputs[f"L0_ffn_{name}"]).reshape(HALVES, P).T)

    def dram(name):
        return nc.dram_tensor(name, arrays[name].shape, F32, kind="ExternalInput").ap()

    out = nc.dram_tensor("out_dram", arrays["x_dram"].shape, F32, kind="ExternalOutput").ap()
    macaron(nc, dram("x_dram"), {name: dram(f"w_{name}_dram") for name in _W},
            dram("mu_r_dram"), dram("mu_k_dram"), out)
    r = run_bass_kernel_spmd(nc, [arrays], core_ids=[0])
    return r.results[0]["out_dram"].reshape(x.shape)
```

```python
from contextlib import ExitStack

import concourse.bass as bass
from concourse import mybir

F32 = mybir.dt.float32
F32R = mybir.dt.float32r
I32 = mybir.dt.int32
ALU = mybir.AluOpType
ACT = mybir.ActivationFunctionType
AX_X = mybir.AxisListType.X

P = 128
D = 256
HALVES = D // P
HEAD = 16
TILES = 4
BLOCK = TILES * P
ROW = TILES * D
BANK = 512
LN_EPS = 1e-5
NORM_EPS = 1e-12
RSQRT_MAGIC = 0x5F3759DF
NEWTON_STEPS = 3
IN_LOOP = 3

WEIGHTS = ("ffn_k", "ffn_r", "ffn_v", "k", "v", "u", "q")
PHASE1_FFN = ("ffn_r", "ffn_v")
PLAIN = ("ffn_r", "ffn_v", "o")


def macaron(nc, x, w_t, mu_r, mu_k, out):
    tokens = x.shape[0]
    batches, seq = 2, tokens // 2
    NB = tokens // BLOCK
    BB = seq // BLOCK
    assert x.shape[1] == D and seq % BLOCK == 0 and NB == batches * BB and BB >= IN_LOOP

    with ExitStack() as ctx:
        def sb(name, shape, dt=F32):
            return ctx.enter_context(nc.sbuf_tensor(name, shape, dt))

        def sem(name):
            return ctx.enter_context(nc.semaphore(name))

        xs = sb("xs", [P, NB * ROW])
        silu_u = sb("silu_u", [P, NB * ROW])
        q_store = sb("q_store", [P, NB * HALVES * BLOCK])
        kv_part = sb("kv_part", [P, NB * D])
        w_raw = silu_u[:, 0:len(WEIGHTS) * HALVES * D].rearrange(
            "p (n c e) -> p n c e", n=len(WEIGHTS), c=HALVES)
        split_both = [n for n in WEIGHTS if n not in PHASE1_FFN]
        w_both = [sb(f"w_{part}", [P, HALVES, len(split_both) * D], F32R) for part in ("hi", "lo")]
        mu = sb("mu", [P, 2, HALVES])
        one_mu = sb("one_mu", [P, 2, HALVES])
        ident = sb("ident", [P, P])
        head_mask = sb("head_mask", [P, P])
        keep = sb("keep", [P, 2 * NB])
        minus_half = sb("minus_half", [P, TILES])
        zeros = sb("zeros", [P, TILES])
        wait_here = sb("wait_here", [P, 5])
        stats = {k: sb("stats" + k, [P, TILES, 6]) for k in "AB"}
        meanvar = {k: sb("meanvar" + k, [P, TILES, 2]) for k in "AB"}
        var_eps = {k: sb("var_eps" + k, [P, TILES]) for k in "AB"}
        neg_mean = {k: sb("neg_mean" + k, [P, TILES]) for k in "AB"}
        rstd = {k: sb("rstd" + k, [P, TILES]) for k in "AB"}
        shift = {k: sb("shift" + k, [P, TILES]) for k in "AB"}
        kv_first = sb("kv_first", [P, D])
        kv_bd = sb("kv_bd", [P, NB * D])
        xn = {"A": sb("xnA", [P, TILES, D]),
              "B": kv_bd[:, 0:ROW].rearrange("p (t d) -> p t d", t=TILES)}
        xt = sb("xt", [P, HALVES, 1 + BLOCK])
        mix = sb("mix", [P, 2, HALVES, BLOCK])
        mix_k_hi = sb("mix_k_hi", [P, HALVES, BLOCK], F32R)
        mix_k_lo = sb("mix_k_lo", [P, HALVES, BLOCK], F32R)
        act_k = sb("act_k", [P, HALVES, BLOCK])
        gate = sb("gate", [P, 2, BANK])
        x2_hi = sb("x2_hi", [P, HALVES, BLOCK], F32R)
        x2_lo = sb("x2_lo", [P, HALVES, BLOCK], F32R)
        k_tok = kv_bd[:, ROW:2 * ROW].rearrange("p (t d) -> p t d", t=TILES)
        v_tok = sb("v_tok", [P, TILES, D])
        q_blk = sb("q_blk", [P, HALVES * BLOCK])
        heads = ROW // HEAD
        head_ss = sb("head_ss", [P, heads])
        head_rn = sb("head_rn", [P, heads])
        head_y = sb("head_y", [P, heads])
        head_t = sb("head_t", [P, heads])
        head_half = head_t[:].bitcast(I32)

        with ExitStack() as phase1_memory:
            def sb1(name, shape):
                return phase1_memory.enter_context(nc.sbuf_tensor(name, shape, F32R))

            w_ffn1 = [sb1(f"w_ffn1_{part}", [P, HALVES, len(PHASE1_FFN) * D]) for part in ("hi", "lo")]
            mix_r_hi = sb1("mix_r_hi", [P, HALVES, BLOCK])
            mix_r_lo = sb1("mix_r_lo", [P, HALVES, BLOCK])
            act_hi = sb1("act_hi", [P, HALVES, BLOCK])
            act_lo = sb1("act_lo", [P, HALVES, BLOCK])
        w_all = sb("w_plain", [P, len(PLAIN), HALVES, D])
        w_plain = {name: w_all[:, n, :, :] for n, name in enumerate(PLAIN)}
        squares = sb("squares", [P, 2, BANK])
        scale_u = sb("scale_u", [P, ROW])
        gout = sb("gout", [P, TILES, D])
        g_t = sb("g_t", [P, HALVES, BLOCK])
        mix_hi, mix_lo = (mix_k_hi, mix_r_hi), (mix_k_lo, mix_r_lo)
        w_parts = {name: (*w_both, slice(n * D, (n + 1) * D)) for n, name in enumerate(split_both)}
        w_parts |= {name: (*w_ffn1, slice(n * D, (n + 1) * D)) for n, name in enumerate(PHASE1_FFN)}

        ps01 = ctx.enter_context(nc.psum_tensor("ps01", [P, 2, BANK], F32))
        ps23 = ctx.enter_context(nc.psum_tensor("ps23", [P, 2, BANK], F32))
        ps45 = ctx.enter_context(nc.psum_tensor("ps45", [P, 2, BANK], F32))
        ps67 = ctx.enter_context(nc.psum_tensor("ps67", [P, 2, BANK], F32))

        s_x_in = sem("s_x_in")
        s_w_in = [sem(f"s_w_in_{n}") for n in WEIGHTS]
        s_mu_in = sem("s_mu_in")
        s_const = sem("s_const")
        s_plain = sem("s_plain")
        s_zero = sem("s_zero")
        s_keep = sem("s_keep")
        s_w_hi = sem("s_w_hi")
        s_w_lo = sem("s_w_lo")
        s_bn = {k: sem("s_bn" + k) for k in "AB"}
        s_mv = {k: sem("s_mv" + k) for k in "AB"}
        s_pool = {k: sem("s_pool" + k) for k in "AB"}
        s_ln = {k: sem("s_ln" + k) for k in "AB"}
        s_xn = {k: sem("s_xn" + k) for k in "AB"}
        s_t = {k: sem("s_t" + k) for k in "AB"}
        s_xn0 = sem("s_xn0")
        s_halo = sem("s_halo")
        s_xt = sem("s_xt")
        s_prev = sem("s_prev")
        s_mix = sem("s_mix")
        s_mix_hi = [sem(f"s_{rk}hi") for rk in "kr"]
        s_mix_lo = [sem(f"s_{rk}lo") for rk in "kr"]
        s_k = sem("s_k")
        s_r = sem("s_r")
        s_relu_k = sem("s_relu_k")
        s_act_k = sem("s_act_k")
        s_act_hi = sem("s_act_hi")
        s_act_lo = sem("s_act_lo")
        s_gate = sem("s_gate")
        s_f = sem("s_f")
        s_gated = sem("s_gated")
        s_x1 = sem("s_x1")
        s_x2_hi = sem("s_x2_hi")
        s_x2_lo = sem("s_x2_lo")
        s_kv = sem("s_kv")
        s_kv_tok = sem("s_kv_tok")
        s_u = sem("s_u")
        s_sig_u = sem("s_sig_u")
        s_silu = sem("s_silu")
        s_q = sem("s_q")
        s_relu_q = sem("s_relu_q")
        s_kvs = sem("s_kvs")
        s_kv_part = sem("s_kv_part")
        s_sum = sem("s_sum")
        s_kv_first = sem("s_kv_first")
        s_kv_bd = sem("s_kv_bd")
        s_q_back = sem("s_q_back")
        s_o = sem("s_o")
        s_sq = sem("s_sq")
        s_ss = sem("s_ss")
        s_newton = sem("s_newton")
        s_rn = sem("s_rn")
        s_scale_0 = sem("s_scale_0")
        s_scale_1 = sem("s_scale_1")
        s_gout = sem("s_gout")
        s_gt = sem("s_gt")
        s_g = sem("s_g")
        s_wo = sem("s_wo")
        s_x2 = sem("s_x2")
        s_x3 = sem("s_x3")
        s_x3_last = sem("s_x3_last")
        s_out = sem("s_out")

        NEWTON_OPS = 3 + 3 * NEWTON_STEPS - 1

        def row(tile, block, start=0, n=ROW):
            return tile[:, bass.ds(block * ROW + start, n)]

        def scale_half(engine, j, n):
            return engine.tensor_tensor(
                scale_u[:, n * BANK:(n + 1) * BANK].rearrange("p (g e) -> p g e", e=HEAD),
                row(silu_u, j, n * BANK, BANK).rearrange("p (g e) -> p g e", e=HEAD),
                head_rn[:, n * heads // 2:(n + 1) * heads // 2].unsqueeze(2).to_broadcast(
                    [P, heads // 2, HEAD]), ALU.mult)

        block = ctx.enter_context(nc.Block())

        def load_weights(eng, which):
            for n in which:
                eng.dma_start(w_raw[:, n, :, :], w_t[WEIGHTS[n]].rearrange("(c p) e -> p c e", p=P)
                              ).then_inc(s_w_in[n], 16)

        @block.sync
        def _(sp):
            def load_x(b):
                if b > 0:
                    sp.wait_ge(s_x_in, b * 16)
                sp.dma_start(row(xs, b).rearrange("p (t d) -> p t d", t=TILES),
                             x[bass.ds(b * BLOCK, BLOCK), :].rearrange("(t p) d -> p t d", p=P)
                             ).then_inc(s_x_in, 16)

            def load_q(j):
                sp.wait_ge(s_relu_q, (j + 1) * HALVES)
                if j > 0:
                    sp.wait_ge(s_o, j * 2)
                sp.dma_start(q_blk[:], row(q_store, j)).then_inc(s_q_back, 16)

            def load_plain(name):
                sp.dma_start(w_plain[name], w_t[name].rearrange("(c p) e -> p c e", p=P)).then_inc(s_plain, 16)

            def store_x(b):
                sp.wait_ge(s_x3, (b + 1) * 2)
                sp.dma_start(out[bass.ds(b * BLOCK, BLOCK), :].rearrange("(t p) d -> p t d", p=P),
                             row(xs, b).rearrange("p (t d) -> p t d", t=TILES)).then_inc(s_out, 16)

            def store_half_of_last(n):
                sp.wait_ge(s_x3_last, n + 1)
                half = BLOCK // 2
                sp.dma_start(out[bass.ds((NB - 1) * BLOCK + n * half, half), :].rearrange("(t p) d -> p t d", p=P),
                             row(xs, NB - 1, n * BANK, BANK).rearrange("p (t d) -> p t d", t=TILES // 2)
                             ).then_inc(s_out, 16)

            load_x(0)
            load_weights(sp, range(2, len(WEIGHTS)))
            for b in range(1, NB):
                load_x(b)
            load_q(0)
            sp.wait_ge(s_f, 2 * NB)
            for name in PLAIN:
                load_plain(name)
            for j in range(1, 3):
                load_q(j)
            for j in range(3, NB):
                load_q(j)
                store_x(j - 3)
            for b in range(NB - 3, NB - 1):
                store_x(b)
            for n in range(2):
                store_half_of_last(n)
            sp.wait_ge(s_out, 16 * (NB + 1))

        @block.gpsimd
        def _(pool):
            nc.gpsimd.memset(ident[:], 0.0).then_inc(s_const, 1)
            nc.gpsimd.memset(head_mask[:], 1.0 / HEAD).then_inc(s_const, 1)
            nc.gpsimd.memset(minus_half[:], -0.5).then_inc(s_const, 1)
            nc.gpsimd.memset(zeros[:], 0.0).then_inc(s_const, 1)
            pool.wait_ge(s_const, 4)
            nc.gpsimd.affine_select(out=ident[:], in_=ident[:], compare_op=ALU.not_equal, fill=1.0, base=0,
                                    pattern=[[-1, P]], channel_multiplier=1).then_inc(s_const, 1)
            by_head = head_mask[:].rearrange("p (h e) -> p h e", e=HEAD)
            nc.gpsimd.affine_select(out=by_head, in_=by_head, compare_op=ALU.is_ge, fill=0.0, base=0,
                                    pattern=[[-HEAD, P // HEAD], [0, HEAD]],
                                    channel_multiplier=1).then_inc(s_const, 1)
            pool.wait_ge(s_const, 6)
            nc.gpsimd.affine_select(out=by_head, in_=by_head, compare_op=ALU.is_ge, fill=0.0, base=HEAD - 1,
                                    pattern=[[HEAD, P // HEAD], [0, HEAD]],
                                    channel_multiplier=-1).then_inc(s_const, 1)

            def ln_scales(kind, n, first=False, second=False):
                pool.wait_ge(s_mv[kind], (n + 1) * TILES)
                nc.gpsimd.tensor_tensor(neg_mean[kind][:], zeros[:], meanvar[kind][:, :, 0],
                                        ALU.subtract).then_inc(s_pool[kind], 1)
                nc.gpsimd.tensor_scalar(var_eps[kind][:], meanvar[kind][:, :, 1], 1.0, LN_EPS,
                                        ALU.mult, ALU.add).then_inc(s_pool[kind], 1)
                pool.wait_ge(s_pool[kind], (n + 1) * 2)
                if not first:
                    pool.wait_ge(s_xn[kind], n * TILES - (2 if kind == "A" else 0))
                    if second:
                        pool.wait_ge(s_xn0, 2)
                nc.gpsimd.tensor_tensor(rstd[kind][:], var_eps[kind][:], minus_half[:],
                                        ALU.pow).then_inc(s_ln[kind], 1)
                pool.wait_ge(s_ln[kind], n * 2 + 1)
                nc.gpsimd.tensor_tensor(shift[kind][:], neg_mean[kind][:], rstd[kind][:],
                                        ALU.mult).then_inc(s_ln[kind], 1)

            def k_low(f, first=False):
                for h in range(HALVES):
                    pool.wait_ge(s_mix_hi[0], f * 2 + h + 1)
                    if not first and h == 0:
                        pool.wait_ge(s_k, f * 2)
                    nc.gpsimd.tensor_tensor(mix_lo[0][:, h, :], mix[:, 0, h, :],
                                            mix_hi[0][:, h, :].bitcast(F32),
                                            ALU.subtract).then_inc(s_mix_lo[0], 1)

            def square_k(f):
                for h in range(HALVES):
                    pool.wait_ge(s_act_hi, f * 2 + h + 1)
                    nc.gpsimd.tensor_tensor(act_k[:, h, :], act_k[:, h, :], act_k[:, h, :],
                                            ALU.mult).then_inc(s_act_k, 1)

            def act_low(f):
                for h in range(HALVES):
                    pool.wait_ge(s_act_k, f * 2 + h + 1)
                    if h == 0:
                        pool.wait_ge(s_f, f * 2)
                    nc.gpsimd.tensor_tensor(act_lo[:, h, :], act_k[:, h, :],
                                            act_hi[:, h, :].bitcast(F32), ALU.subtract).then_inc(s_act_lo, 1)

            def scale_second_gate(j, first=False):
                pool.wait_ge(s_rn, j + 1)
                if not first:
                    pool.wait_ge(s_gout, j * 2)
                scale_half(nc.gpsimd, j, 1).then_inc(s_scale_1, 1)

            def add_ffn2(f):
                b = f - NB
                for n in range(2):
                    pool.wait_ge(s_gated, f * 2 + n + 1)
                    xb = row(xs, b, n * BANK, BANK)
                    nc.gpsimd.tensor_tensor(xb, xb, gate[:, n, :], ALU.add).then_inc(s_x3, 1)

            ln_scales("A", 0, first=True)
            k_low(0, first=True)
            ln_scales("A", 1, second=True)
            k_low(1)
            ln_scales("B", 0, first=True)
            with pool.Fori(1, NB - 1) as i:
                ln_scales("A", i + 1)
                square_k(i)
                act_low(i)
                k_low(i + 1)
                ln_scales("B", i)
            square_k(NB - 1)
            act_low(NB - 1)
            ln_scales("B", NB - 1)
            scale_second_gate(0, first=True)
            ln_scales("A", NB)
            scale_second_gate(1)
            with pool.Fori(2, NB) as j:
                k_low(j + (NB - 2))
                ln_scales("A", j + (NB - 1))
                scale_second_gate(j)
                add_ffn2(j + (NB - 2))
            k_low(2 * NB - 2)
            ln_scales("A", 2 * NB - 1)
            add_ffn2(2 * NB - 2)
            k_low(2 * NB - 1)

        @block.scalar
        def _(act):
            load_weights(act, range(2))
            act.dma_start(mu[:, 0, :], mu_k).then_inc(s_mu_in, 16)
            act.dma_start(mu[:, 1, :], mu_r).then_inc(s_mu_in, 16)

            def split_weights(lo, hi):
                for n in range(lo, hi):
                    act.wait_ge(s_w_in[n], 16)
                    w_hi, _, cols = w_parts[WEIGHTS[n]]
                    nc.scalar.activation(w_hi[:, :, cols], w_raw[:, n, :, :], ACT.Identity,
                                         scale=0.5 if WEIGHTS[n] == "ffn_v" else 1.0).then_inc(s_w_hi, 1)

            def normalize(kind, n, b, first=False, tiles=range(TILES)):
                act.wait_ge(s_ln[kind], (n + 1) * 2)
                if not first:
                    act.wait_ge(s_t[kind], n * HALVES)
                for t in tiles:
                    nc.scalar.activation(xn[kind][:, t, :], row(xs, b, t * D, D), ACT.Identity,
                                         bias=shift[kind][:, t:t + 1],
                                         scale=rstd[kind][:, t:t + 1]).then_inc(s_xn[kind], 1)

            def previous(f, rk, h):
                act.wait_ge(s_xt, f * 2 + h + 1)
                nc.scalar.activation(mix[:, rk, h, :], xt[:, h, 0:BLOCK], ACT.Copy,
                                     scale=one_mu[:, rk, h:h + 1]).then_inc(s_prev, 1)

            def keep_last(f):
                act.wait_ge(s_mix, f * 4)
                nc.scalar.activation(xt[:, :, 0:1], xt[:, :, BLOCK:BLOCK + 1], ACT.Copy,
                                     scale=keep[:, bass.ds(f, 1)]).then_inc(s_halo, 1)

            def previous_k(f, h, ps=ps23, first=False):
                if h == 0 and first:
                    act.wait_ge(s_keep, 4)
                elif h == 0:
                    act.wait_ge(s_halo, f * 1)
                    act.wait_ge(s_mix_lo[0], f * 2)
                act.wait_ge(s_t["A"], f * 2 + h + 1)
                nc.scalar.activation(xt[:, h, 1:1 + BLOCK], ps[:, h, :], ACT.Identity).then_inc(s_xt, 1)
                previous(f, 0, h)

            def previous_r(f, s_used=None):
                if s_used is not None:
                    act.wait_ge(s_used, f * 2)
                for h in range(HALVES):
                    previous(f, 1, h)

            def mix_high(f, rk, first=False):
                if not first:
                    act.wait_ge((s_k, s_r)[rk], f * 2)
                for h in range(HALVES):
                    act.wait_ge(s_mix, f * 4 + rk * 2 + h + 1)
                    nc.scalar.activation(mix_hi[rk][:, h, :], mix[:, rk, h, :],
                                         ACT.Identity).then_inc(s_mix_hi[rk], 1)

            def relu_k(f, h, s_relu_used=None, s_high_used=None):
                act.wait_ge(s_k, f * 2 + h + 1)
                if s_relu_used is not None:
                    act.wait_ge(s_relu_used, f * 2)
                nc.scalar.activation(act_k[:, h, :], ps23[:, h, :], ACT.Relu).then_inc(s_relu_k, 1)
                act.wait_ge(s_relu_k, f * 2 + h + 1)
                if s_high_used is not None:
                    act.wait_ge(s_high_used, f * 2)
                nc.scalar.activation(act_hi[:, h, :], act_k[:, h, :], ACT.Square).then_inc(s_act_hi, 1)

            def activate_k_plain(f):
                act.wait_ge(s_f, f * 2)
                for h in range(HALVES):
                    act.wait_ge(s_k, f * 2 + h + 1)
                    nc.scalar.activation(act_k[:, h, :], ps23[:, h, :], ACT.Relu).then_inc(s_relu_k, 1)
                    act.wait_ge(s_relu_k, f * 2 + h + 1)
                    nc.scalar.activation(act_k[:, h, :], act_k[:, h, :], ACT.Square).then_inc(s_act_k, 1)

            def sigmoid_r(f, n, s_added=None, added=0):
                act.wait_ge(s_r, f * 2 + n + 1)
                if s_added is not None and n == 0:
                    act.wait_ge(s_added, added)
                nc.scalar.activation(gate[:, n, :], ps45[:, n, :], ACT.Sigmoid).then_inc(s_gate, 1)

            def x2_high(a, ps=ps01, first=False):
                for h in range(HALVES):
                    act.wait_ge(s_t["B"], a * 2 + h + 1)
                    if not first and h == 0:
                        act.wait_ge(s_q, a * 2)
                    nc.scalar.activation(x2_hi[:, h, :], ps[:, h, :], ACT.Identity).then_inc(s_x2_hi, 1)

            def sigmoid_u(a, first=False):
                for n in range(2):
                    act.wait_ge(s_u, a * 2 + n + 1)
                    if first and n == 0:
                        act.wait_ge(s_w_lo, len(WEIGHTS))
                    nc.scalar.activation(row(silu_u, a, n * BANK, BANK), ps01[:, n, :], ACT.Sigmoid).then_inc(s_sig_u, 1)

            def relu_q(a):
                for h in range(HALVES):
                    act.wait_ge(s_q, a * 2 + h + 1)
                    nc.scalar.activation(row(q_store, a, h * BLOCK, BLOCK), ps67[:, h, :],
                                         ACT.Relu).then_inc(s_relu_q, 1)

            def square_heads(j, ps=ps67, first=False):
                for n in range(2):
                    act.wait_ge(s_o, j * 2 + n + 1)
                    if not first and n == 0:
                        act.wait_ge(s_ss, j * 2)
                    nc.scalar.activation(squares[:, n, :], ps[:, n, :], ACT.Square,
                                         scale=float(HEAD) ** -0.5).then_inc(s_sq, 1)

            def copy_g(j, ps=ps01, first=False):
                for h in range(HALVES):
                    act.wait_ge(s_gt, j * 2 + h + 1)
                    if not first and h == 0:
                        act.wait_ge(s_wo, j * 2)
                    nc.scalar.activation(g_t[:, h, :], ps[:, h, :], ACT.Identity).then_inc(s_g, 1)

            act.wait_ge(s_zero, 1)
            nc.scalar.activation(wait_here[:, 4:5], wait_here[:, 4:5], ACT.Sigmoid)
            split_weights(0, 2)
            normalize("A", 0, 0, first=True, tiles=(0, 1))
            previous_k(0, 0, first=True)
            previous_k(0, 1)
            mix_high(0, 0, first=True)
            previous_r(0)
            split_weights(2, 3)
            mix_high(0, 1, first=True)
            relu_k(0, 0)
            relu_k(0, 1)
            normalize("A", 1, 1)
            sigmoid_r(0, 0)
            sigmoid_r(0, 1)
            keep_last(1)
            previous_k(1, 0)
            previous_k(1, 1)
            previous_r(1, s_mix_lo[1])
            mix_high(1, 0)
            mix_high(1, 1)
            split_weights(3, len(WEIGHTS))
            normalize("B", 0, 0, first=True)

            def phase1(i, first=False):
                relu_k(i, 0, s_act_lo, s_f)
                x2_high(i - 1, first=first)
                relu_k(i, 1)
                sigmoid_r(i, 0, s_x1, i * 2)
                sigmoid_r(i, 1)
                keep_last(i + 1)
                normalize("A", i + 1, i + 1)
                previous_k(i + 1, 0)
                previous_k(i + 1, 1)
                previous_r(i + 1, s_mix_lo[1])
                mix_high(i + 1, 0)
                sigmoid_u(i - 1, first=first)
                mix_high(i + 1, 1)
                normalize("B", i, i)
                relu_q(i - 1)

            phase1(1, first=True)
            with act.Fori(2, NB - 1) as i:
                phase1(i)
            relu_k(NB - 1, 0, s_act_lo, s_f)
            x2_high(NB - 2)
            relu_k(NB - 1, 1)
            sigmoid_r(NB - 1, 0, s_x1, 2 * (NB - 1))
            sigmoid_r(NB - 1, 1)
            square_heads(0, ps23, first=True)
            sigmoid_u(NB - 2)
            normalize("B", NB - 1, NB - 1)
            relu_q(NB - 2)
            x2_high(NB - 1, ps45)
            copy_g(0, ps23, first=True)
            sigmoid_u(NB - 1)
            square_heads(1, ps23)
            keep_last(NB)
            normalize("A", NB, 0)
            relu_q(NB - 1)
            previous_k(NB, 0, ps45)
            previous_k(NB, 1, ps45)
            copy_g(1)
            mix_high(NB, 0)
            previous_r(NB, s_r)
            square_heads(2)

            def phase2(j, s_added, added, last=False):
                activate_k_plain(j + (NB - 2))
                sigmoid_r(j + (NB - 2), 0, s_added, added)
                keep_last(j + (NB - 1))
                normalize("A", j + (NB - 1), j - 1)
                sigmoid_r(j + (NB - 2), 1)
                previous_k(j + (NB - 1), 0)
                copy_g(j)
                previous_k(j + (NB - 1), 1)
                mix_high(j + (NB - 1), 0)
                previous_r(j + (NB - 1), s_r)
                if not last:
                    square_heads(j + 1)

            phase2(2, s_x1, 2 * NB)
            with act.Fori(3, NB - 1) as j:
                phase2(j, s_x3, (j - 2) * 2)
            phase2(NB - 1, s_x3, 2 * (NB - 3), last=True)
            activate_k_plain(2 * NB - 2)
            sigmoid_r(2 * NB - 2, 0, s_x3, 2 * (NB - 2))
            keep_last(2 * NB - 1)
            normalize("A", 2 * NB - 1, NB - 1)
            sigmoid_r(2 * NB - 2, 1)
            previous_k(2 * NB - 1, 0)
            previous_k(2 * NB - 1, 1)
            mix_high(2 * NB - 1, 0)
            previous_r(2 * NB - 1, s_r)
            activate_k_plain(2 * NB - 1)
            sigmoid_r(2 * NB - 1, 0, s_x3, 2 * (NB - 1))
            sigmoid_r(2 * NB - 1, 1)

        @block.vector
        def _(dve):
            nc.vector.memset(wait_here[:, 4:5], 0.0).then_inc(s_zero, 1)
            nc.vector.memset(keep[:], 1.0).then_inc(s_keep, 1)
            nc.vector.memset(xt[:, :, 0:1], 0.0).then_inc(s_keep, 1)
            dve.wait_ge(s_keep, 2)
            nc.vector.memset(keep[:, 0:2 * NB:BB], 0.0).then_inc(s_keep, 1)

            def split_weights(lo, hi):
                for n in range(lo, hi):
                    dve.wait_ge(s_w_hi, n + 1)
                    w_hi, w_lo, cols = w_parts[WEIGHTS[n]]
                    nc.vector.scalar_tensor_tensor(
                        out=w_lo[:, :, cols], in0=w_raw[:, n, :, :],
                        scalar=0.5 if WEIGHTS[n] == "ffn_v" else 1.0,
                        in1=w_hi[:, :, cols].bitcast(F32), op0=ALU.mult, op1=ALU.subtract).then_inc(s_w_lo, 1)

            def ln_stats(kind, n, b, first=False):
                col = 2 * "AB".index(kind)
                if not first:
                    dve.wait_ge(s_mv[kind], n * TILES)
                nc.vector.memset(wait_here[:, col:col + 1], 0.0)
                for t in range(TILES):
                    nc.vector.bn_stats(stats[kind][:, t, :], row(xs, b, t * D, D)).then_inc(s_bn[kind], 1)
                if not first:
                    dve.wait_ge(s_ln[kind], n * 2)
                dve.wait_ge(s_bn[kind], (n + 1) * TILES)
                nc.vector.memset(wait_here[:, col + 1:col + 2], 0.0)
                for t in range(TILES):
                    nc.vector.bn_aggr(meanvar[kind][:, t, :], stats[kind][:, t, :]).then_inc(s_mv[kind], 1)

            def mix_current(rk, f):
                for h in range(HALVES):
                    dve.wait_ge(s_prev, f * 4 + rk * 2 + h + 1)
                    m = mix[:, rk, h, :]
                    nc.vector.scalar_tensor_tensor(out=m, in0=xt[:, h, 1:1 + BLOCK], scalar=mu[:, rk, h:h + 1],
                                                   in1=m, op0=ALU.mult, op1=ALU.add).then_inc(s_mix, 1)

            def r_low(f, first=False):
                if not first:
                    dve.wait_ge(s_r, f * 2)
                for h in range(HALVES):
                    dve.wait_ge(s_mix_hi[1], f * 2 + h + 1)
                    nc.vector.tensor_tensor(mix_lo[1][:, h, :], mix[:, 1, h, :],
                                            mix_hi[1][:, h, :].bitcast(F32),
                                            ALU.subtract).then_inc(s_mix_lo[1], 1)

            def gate_ffn(f, half=False, added=False):
                for n in range(2):
                    dve.wait_ge(s_f, f * 2 + n + 1)
                    dve.wait_ge(s_gate, f * 2 + n + 1)
                    if half:
                        gated = nc.vector.scalar_tensor_tensor(out=gate[:, n, :], in0=ps45[:, n, :], scalar=0.5,
                                                               in1=gate[:, n, :], op0=ALU.mult, op1=ALU.mult)
                    else:
                        gated = nc.vector.tensor_tensor(gate[:, n, :], ps45[:, n, :], gate[:, n, :], ALU.mult)
                    gated.then_inc(s_gated, 1)
                    if added:
                        dve.wait_ge(s_gated, f * 2 + n + 1)
                        xb = row(xs, f - NB, n * BANK, BANK)
                        nc.vector.tensor_tensor(xb, xb, gate[:, n, :], ALU.add).then_inc(s_x3_last, 1)

            def add_ffn1(f):
                for n in range(2):
                    dve.wait_ge(s_gated, f * 2 + n + 1)
                    xb = row(xs, f, n * BANK, BANK)
                    nc.vector.tensor_tensor(xb, xb, gate[:, n, :], ALU.add).then_inc(s_x1, 1)

            def x2_low(a, ps=ps01):
                for h in range(HALVES):
                    dve.wait_ge(s_x2_hi, a * 2 + h + 1)
                    nc.vector.tensor_tensor(x2_lo[:, h, :], ps[:, h, :], x2_hi[:, h, :].bitcast(F32),
                                            ALU.subtract).then_inc(s_x2_lo, 1)

            def keep_kv(a, first=False):
                for t in range(TILES):
                    dve.wait_ge(s_kv, a * TILES + t + 1)
                    if not first and t == 0:
                        dve.wait_ge(s_kvs, a * 1)
                    nc.vector.tensor_copy(v_tok[:, t, :], ps67[:, t % 2, D:2 * D]).then_inc(s_kv_tok, 1)
                    nc.vector.tensor_scalar(k_tok[:, t, :], ps67[:, t % 2, 0:D], 0.0, None,
                                            ALU.max).then_inc(s_kv_tok, 1)

            def silu(a, n):
                dve.wait_ge(s_sig_u, a * 2 + n + 1)
                su = row(silu_u, a, n * BANK, BANK)
                nc.vector.tensor_tensor(su, ps01[:, n, :], su, ALU.mult).then_inc(s_silu, 1)

            def keep_kv_part(a):
                dve.wait_ge(s_kvs, a + 1)
                nc.vector.tensor_copy(kv_part[:, bass.ds(a * D, D)], ps01[:, 0, 0:D]).then_inc(s_kv_part, 1)

            def sum_kv(batch, blocks):
                first = batch * BB
                total = kv_part[:, first * D:(first + 1) * D]
                dve.wait_ge(s_kv_part, first + blocks[-1] + 1)
                for n in blocks:
                    if n > 1:
                        dve.wait_ge(s_sum, batch * (BB - 1) + n - 1)
                    part = kv_part[:, (first + n) * D:(first + n + 1) * D]
                    nc.vector.tensor_tensor(total, total, part, ALU.add).then_inc(s_sum, 1)

            def diagonal_kv(batch, dst):
                return nc.vector.tensor_tensor(
                    dst.rearrange("p (h e) -> p h e", h=HALVES),
                    kv_part[:, batch * BB * D:(batch * BB + 1) * D].rearrange("p (h e) -> p h e", h=HALVES),
                    head_mask[:].unsqueeze(1).to_broadcast([P, HALVES, P]), ALU.mult)

            def keep_kv_of_first():
                dve.wait_ge(s_sum, BB - 1)
                dve.wait_ge(s_const, 7)
                diagonal_kv(0, kv_first[:]).then_inc(s_kv_first, 1)

            def place_kv():
                dve.wait_ge(s_sum, 2 * (BB - 1))
                dve.wait_ge(s_t["B"], 2 * NB)
                dve.wait_ge(s_kvs, NB)
                for j in range(IN_LOOP, NB):
                    diagonal_kv(j // BB, kv_bd[:, j * D:(j + 1) * D]).then_inc(s_kv_bd, 1)

            def add_attention(j, ps=ps01):
                for n in range(2):
                    dve.wait_ge(s_wo, j * 2 + n + 1)
                    xb = row(xs, j, n * BANK, BANK)
                    nc.vector.tensor_tensor(xb, xb, ps[:, n, :], ALU.add).then_inc(s_x2, 1)

            def head_norms(j, first=False):
                for n in range(2):
                    dve.wait_ge(s_sq, j * 2 + n + 1)
                    nc.vector.tensor_reduce(head_ss[:, n * heads // 2:(n + 1) * heads // 2],
                                            squares[:, n, :].rearrange("p (g e) -> p g e", e=HEAD),
                                            AX_X, ALU.add).then_inc(s_ss, 1)
                dve.wait_ge(s_ss, (j + 1) * 2)
                step = [0]

                def then(ins):
                    step[0] += 1
                    ins.then_inc(s_newton, 1)
                    dve.wait_ge(s_newton, j * NEWTON_OPS + step[0])

                then(nc.vector.tensor_scalar(head_ss[:], head_ss[:], NORM_EPS ** 2, None, ALU.max))
                then(nc.vector.tensor_scalar(head_half, head_ss[:].bitcast(I32), 1, None,
                                             ALU.arith_shift_right))
                then(nc.vector.tensor_scalar(head_y[:].bitcast(I32), head_half, -1.0, float(RSQRT_MAGIC),
                                             ALU.mult, ALU.add))
                if not first:
                    dve.wait_ge(s_scale_1, j * 1)
                for n in range(NEWTON_STEPS):
                    last = n == NEWTON_STEPS - 1
                    then(nc.vector.tensor_tensor(head_t[:], head_y[:], head_y[:], ALU.mult))
                    then(nc.vector.scalar_tensor_tensor(out=head_t[:], in0=head_t[:], scalar=-0.5,
                                                        in1=head_ss[:], op0=ALU.mult, op1=ALU.mult))
                    y = nc.vector.scalar_tensor_tensor(out=head_rn[:] if last else head_y[:], in0=head_t[:],
                                                       scalar=1.5, in1=head_y[:], op0=ALU.add, op1=ALU.mult)
                    if last:
                        y.then_inc(s_rn, 1)
                    else:
                        then(y)
                assert step[0] == NEWTON_OPS

            def gate_heads(j, ps=ps67, first=False):
                dve.wait_ge(s_rn, j + 1)
                if not first:
                    dve.wait_ge(s_gout, j * 2)
                scale_half(nc.vector, j, 0).then_inc(s_scale_0, 1)
                if not first:
                    dve.wait_ge(s_gt, j * 2)
                for n in range(2):
                    dve.wait_ge((s_scale_0, s_scale_1)[n], j + 1)
                    nc.vector.tensor_tensor(gout[:, 2 * n:2 * n + 2, :],
                                            ps[:, n, :].rearrange("p (t d) -> p t d", t=2),
                                            scale_u[:, n * BANK:(n + 1) * BANK].rearrange("p (t d) -> p t d", t=2),
                                            ALU.mult).then_inc(s_gout, 1)

            def stats_of_input(f, first=False):
                dve.wait_ge(s_x_in, (f + 1) * 16)
                ln_stats("A", f, f, first=first)

            def stats_of_x1(a, first=False):
                dve.wait_ge(s_x1, (a + 1) * 2)
                ln_stats("B", a, a, first=first)

            def stats_of_x2(f, b):
                dve.wait_ge(s_x2, (b + 1) * 2)
                ln_stats("A", f, b)

            def square_first_k():
                for h in range(HALVES):
                    dve.wait_ge(s_act_hi, h + 1)
                    nc.vector.tensor_tensor(act_k[:, h, :], act_k[:, h, :], act_k[:, h, :],
                                            ALU.mult).then_inc(s_act_k, 1)
                    dve.wait_ge(s_act_k, h + 1)
                    nc.vector.tensor_tensor(act_lo[:, h, :], act_k[:, h, :], act_hi[:, h, :].bitcast(F32),
                                            ALU.subtract).then_inc(s_act_lo, 1)

            stats_of_input(0, first=True)
            dve.wait_ge(s_ln["A"], 2)
            for t in (2, 3):
                nc.vector.tensor_scalar(xn["A"][:, t, :], row(xs, 0, t * D, D), rstd["A"][:, t:t + 1],
                                        shift["A"][:, t:t + 1], ALU.mult, ALU.add).then_inc(s_xn0, 1)
            dve.wait_ge(s_mu_in, 32)
            nc.vector.tensor_scalar(one_mu[:], mu[:], -1.0, 1.0, ALU.mult, ALU.add).then_inc(s_keep, 1)
            split_weights(0, 2)
            mix_current(0, 0)
            stats_of_input(1)
            mix_current(1, 0)
            r_low(0, first=True)
            split_weights(2, 3)
            square_first_k()
            mix_current(0, 1)
            gate_ffn(0)
            add_ffn1(0)
            mix_current(1, 1)
            stats_of_x1(0, first=True)
            r_low(1)
            split_weights(3, len(WEIGHTS))

            def phase1(i, first=False):
                stats_of_input(i + 1)
                x2_low(i - 1)
                keep_kv(i - 1, first=first)
                mix_current(0, i + 1)
                gate_ffn(i)
                add_ffn1(i)
                silu(i - 1, 0)
                stats_of_x1(i)
                mix_current(1, i + 1)
                silu(i - 1, 1)
                r_low(i + 1)
                keep_kv_part(i - 1)

            phase1(1, first=True)
            with dve.Fori(2, NB - 1) as i:
                phase1(i)
            sum_kv(0, range(1, BB))
            keep_kv_of_first()
            x2_low(NB - 2)
            keep_kv(NB - 2)
            gate_ffn(NB - 1)
            add_ffn1(NB - 1)
            stats_of_x1(NB - 1)
            silu(NB - 2, 0)
            silu(NB - 2, 1)
            head_norms(0, first=True)
            x2_low(NB - 1, ps45)
            keep_kv_part(NB - 2)
            gate_heads(0, ps23, first=True)
            sum_kv(1, range(1, BB - 1))
            keep_kv(NB - 1)
            silu(NB - 1, 0)
            silu(NB - 1, 1)
            add_attention(0, ps45)
            stats_of_x2(NB, 0)
            head_norms(1)
            keep_kv_part(NB - 1)
            gate_heads(1, ps23)

            def phase2(j, first=False):
                mix_current(0, j + (NB - 2))
                mix_current(1, j + (NB - 2))
                if first:
                    sum_kv(1, range(BB - 1, BB))
                    place_kv()
                add_attention(j - 1)
                stats_of_x2(j + (NB - 1), j - 1)
                head_norms(j)
                gate_heads(j)
                gate_ffn(j + (NB - 2), half=True)

            phase2(2, first=True)
            with dve.Fori(3, NB) as j:
                phase2(j)
            mix_current(0, 2 * NB - 2)
            mix_current(1, 2 * NB - 2)
            add_attention(NB - 1)
            stats_of_x2(2 * NB - 1, NB - 1)
            gate_ffn(2 * NB - 2, half=True)
            mix_current(0, 2 * NB - 1)
            mix_current(1, 2 * NB - 1)
            gate_ffn(2 * NB - 1, half=True, added=True)

        @block.tensor
        def _(pe):
            def product(dst, a_hi, a_lo, b_hi, b_lo, start, stop):
                nc.tensor.matmul(dst, a_hi, b_hi, start=start, stop=False)
                nc.tensor.matmul(dst, a_hi, b_lo, start=False, stop=False)
                return nc.tensor.matmul(dst, a_lo, b_hi, start=False, stop=stop)

            def weight(name, c, start=0, n=D):
                w_hi, w_lo, cols = w_parts[name]
                cols = slice(cols.start + start, cols.start + start + n)
                return w_hi[:, c, cols], w_lo[:, c, cols]

            def token_rows(hi, lo, c, t):
                cols = slice(t * P, (t + 1) * P)
                return hi[:, c, cols], lo[:, c, cols]

            def to_features(kind, n, ps, first=False):
                for h in range(HALVES):
                    for t in range(TILES):
                        if h == 0 and kind == "A":
                            if first and t >= 2:
                                pe.wait_ge(s_xn0, t - 1)
                            else:
                                pe.wait_ge(s_xn[kind], t + 1 if first else n * TILES + t - 1)
                        elif h == 0:
                            pe.wait_ge(s_xn[kind], n * TILES + t + 1)
                        last = nc.tensor.transpose(ps[:, h, t * P:(t + 1) * P],
                                                   xn[kind][:, t, h * P:(h + 1) * P], ident[:])
                    last.then_inc(s_t[kind], 1)

            def transpose_a(f, first=False):
                if not first:
                    pe.wait_ge(s_relu_k, f * 2)
                to_features("A", f, ps23, first=first)

            def ffn_k(f):
                for m in range(HALVES):
                    for c in range(HALVES):
                        if m == 0:
                            pe.wait_ge(s_mix_hi[0], f * 2 + c + 1)
                            pe.wait_ge(s_mix_lo[0], f * 2 + c + 1)
                        last = product(ps23[:, m, :], *weight("ffn_k", c, m * P, P),
                                       mix_hi[0][:, c, :], mix_lo[0][:, c, :], c == 0, c == HALVES - 1)
                    last.then_inc(s_k, 1)

            def by_tiles(ps, hi, lo, name, s_done, s_free=None, free=0, tiles=range(TILES)):
                for t in tiles:
                    if t % 2 == 0 and s_free is not None:
                        pe.wait_ge(s_free, free + t // 2)
                    for c in range(HALVES):
                        last = product(ps[:, t // 2, (t % 2) * D:(t % 2 + 1) * D], *token_rows(hi, lo, c, t),
                                       *weight(name, c), c == 0, c == HALVES - 1)
                    if t % 2:
                        last.then_inc(s_done, 1)

            def by_tiles_plain(ps, operand, name, s_done, s_free=None, free=0, tiles=range(TILES)):
                for t in tiles:
                    if t % 2 == 0 and s_free is not None:
                        pe.wait_ge(s_free, free + t // 2)
                    for c in range(HALVES):
                        last = nc.tensor.matmul(ps[:, t // 2, (t % 2) * D:(t % 2 + 1) * D],
                                                operand[:, c, t * P:(t + 1) * P], w_plain[name][:, c, :],
                                                start=(c == 0), stop=(c == HALVES - 1))
                    if t % 2:
                        last.then_inc(s_done, 1)

            def ffn_r_plain(f):
                pe.wait_ge(s_mix, f * 4 + 4)
                pe.wait_ge(s_gated, f * 2)
                by_tiles_plain(ps45, mix[:, 1, :, :], "ffn_r", s_r)

            def ffn_v_plain(f, tiles=range(TILES)):
                if 0 in tiles:
                    pe.wait_ge(s_act_k, f * 2 + 2)
                by_tiles_plain(ps45, act_k, "ffn_v", s_f, s_gate, f * 2 + 1, tiles)

            def ffn_r(f, first=False, tiles=range(TILES)):
                if 0 in tiles:
                    pe.wait_ge(s_mix_hi[1], f * 2 + 2)
                    pe.wait_ge(s_mix_lo[1], f * 2 + 2)
                    if not first:
                        pe.wait_ge(s_gated, f * 2)
                by_tiles(ps45, mix_hi[1], mix_lo[1], "ffn_r", s_r, tiles=tiles)

            def ffn_v(f):
                pe.wait_ge(s_act_hi, f * 2 + 2)
                pe.wait_ge(s_act_lo, f * 2 + 2)
                by_tiles(ps45, act_hi, act_lo, "ffn_v", s_f, s_gate, f * 2 + 1)

            def wait_ps01(a):
                pe.wait_ge(s_kv_part, a * 1)
                pe.wait_ge(s_silu, a * 2)

            def transpose_b(a, first=False):
                if not first:
                    wait_ps01(a)
                to_features("B", a, ps01)

            def kv_of_tokens(a, first=False):
                if not first:
                    pe.wait_ge(s_relu_q, a * 2)
                for t in range(TILES):
                    if t >= 2:
                        pe.wait_ge(s_kv_tok, a * 8 + 2 * (t - 1))
                    for c in range(HALVES):
                        if t == 0:
                            pe.wait_ge(s_x2_hi, a * 2 + c + 1)
                            pe.wait_ge(s_x2_lo, a * 2 + c + 1)
                        last = product(ps67[:, t % 2, :], *token_rows(x2_hi, x2_lo, c, t),
                                       *weight("k", c, 0, 2 * D), c == 0, c == HALVES - 1)
                    last.then_inc(s_kv, 1)

            def u_of_tokens(a):
                by_tiles(ps01, x2_hi, x2_lo, "u", s_u)

            def q_of_tokens(a):
                pe.wait_ge(s_kv_tok, a * 8 + 8)
                for m in range(HALVES):
                    for c in range(HALVES):
                        last = product(ps67[:, m, :], *weight("q", c, m * P, P),
                                       x2_hi[:, c, :], x2_lo[:, c, :], c == 0, c == HALVES - 1)
                    last.then_inc(s_q, 1)

            def sum_kv_of_block(a):
                pe.wait_ge(s_kv_tok, a * 8 + 8)
                pe.wait_ge(s_silu, a * 2 + 1)
                for h in range(HALVES):
                    half = slice(h * P, (h + 1) * P)
                    for t in range(TILES):
                        last = nc.tensor.matmul(ps01[:, 0, half], k_tok[:, t, half], v_tok[:, t, half],
                                                start=(t == 0), stop=(t == TILES - 1))
                last.then_inc(s_kvs, 1)

            def attend(j, ps, kv, at):
                pe.wait_ge(s_q_back, (j + 1) * 16)
                for t in range(TILES):
                    for h in range(HALVES):
                        last = nc.tensor.matmul(
                            ps[:, t // 2, (t % 2) * D + h * P:(t % 2) * D + (h + 1) * P],
                            q_blk[:, h * BLOCK + t * P:h * BLOCK + (t + 1) * P],
                            kv[:, bass.ds(at + h * P, P)], start=True, stop=True)
                    if t % 2:
                        last.then_inc(s_o, 1)

            def transpose_g(j, ps=ps01):
                for n in range(2):
                    pe.wait_ge(s_gout, j * 2 + n + 1)
                    for h in range(HALVES):
                        for t in (2 * n, 2 * n + 1):
                            last = nc.tensor.transpose(ps[:, h, t * P:(t + 1) * P],
                                                       gout[:, t, h * P:(h + 1) * P], ident[:])
                        if n == 1:
                            last.then_inc(s_gt, 1)

            def project_out(j, ps=ps01):
                pe.wait_ge(s_g, j * 2 + 2)
                by_tiles_plain(ps, g_t, "o", s_wo)

            def keep_clock_up(n):
                for _ in range(n):
                    nc.tensor.transpose(ps67[:, 0, 0:P], ident[:], ident[:])

            pe.wait_ge(s_const, 7)
            keep_clock_up(32)
            transpose_a(0, first=True)
            keep_clock_up(38)
            pe.wait_ge(s_w_lo, 2)
            ffn_k(0)
            ffn_r(0, first=True)
            transpose_a(1)
            pe.wait_ge(s_w_lo, 3)
            ffn_v(0)
            keep_clock_up(20)

            def phase1(i, first=False):
                ffn_k(i)
                ffn_r(i, tiles=(0, 1))
                transpose_b(i - 1, first=first)
                ffn_r(i, tiles=(2, 3))
                if first:
                    pe.wait_ge(s_w_lo, len(WEIGHTS))
                kv_of_tokens(i - 1, first=first)
                transpose_a(i + 1)
                ffn_v(i)
                u_of_tokens(i - 1)
                q_of_tokens(i - 1)
                sum_kv_of_block(i - 1)

            phase1(1, first=True)
            with pe.Fori(2, NB - 1) as i:
                phase1(i)
            ffn_k(NB - 1)
            ffn_r(NB - 1, tiles=(0, 1))
            transpose_b(NB - 2)
            ffn_r(NB - 1, tiles=(2, 3))
            kv_of_tokens(NB - 2)
            ffn_v(NB - 1)
            pe.wait_ge(s_kv_first, 1)
            pe.wait_ge(s_relu_k, 2 * NB)
            attend(0, ps23, kv_first, 0)
            u_of_tokens(NB - 2)
            q_of_tokens(NB - 2)
            pe.wait_ge(s_gated, 2 * NB)
            to_features("B", NB - 1, ps45)
            sum_kv_of_block(NB - 2)
            kv_of_tokens(NB - 1)
            transpose_g(0, ps23)
            wait_ps01(NB - 1)
            u_of_tokens(NB - 1)
            pe.wait_ge(s_g, 2)
            pe.wait_ge(s_plain, 16 * len(PLAIN))
            project_out(0, ps45)
            attend(1, ps23, kv_first, 0)
            q_of_tokens(NB - 1)
            sum_kv_of_block(NB - 1)
            pe.wait_ge(s_x2, 2)
            to_features("A", NB, ps45)
            pe.wait_ge(s_relu_q, 2 * NB)
            attend(2, ps67, kv_first, 0)
            wait_ps01(NB)
            transpose_g(1)
            project_out(1)

            def phase2(j, last=False):
                ffn_k(j + (NB - 2))
                ffn_r_plain(j + (NB - 2))
                ffn_v_plain(j + (NB - 2), tiles=(0, 1))
                transpose_a(j + (NB - 1))
                ffn_v_plain(j + (NB - 2), tiles=(2, 3))
                pe.wait_ge(s_x2, j * 2)
                transpose_g(j)
                if not last:
                    pe.wait_ge(s_kv_bd, NB - IN_LOOP)
                    attend(j + 1, ps67, kv_bd, (j + 1) * D)
                project_out(j)

            with pe.Fori(2, NB - 1) as j:
                phase2(j)
            phase2(NB - 1, last=True)
            ffn_k(2 * NB - 2)
            ffn_r_plain(2 * NB - 2)
            ffn_v_plain(2 * NB - 2, tiles=(0, 1))
            transpose_a(2 * NB - 1)
            ffn_v_plain(2 * NB - 2, tiles=(2, 3))
            keep_clock_up(20)
            ffn_k(2 * NB - 1)
            ffn_r_plain(2 * NB - 1)
            ffn_v_plain(2 * NB - 1)


_W = {"ffn_k": "L0_ffn_W_k", "ffn_r": "L0_ffn_W_r", "ffn_v": "L0_ffn_W_v", "k": "L0_attn_Wk",
      "v": "L0_attn_Wv", "u": "L0_attn_Wu", "q": "L0_attn_Wq", "o": "L0_attn_Wo"}


def kernel(**inputs):
    import numpy as np
    import concourse.bacc as bacc
    from concourse.bass_utils import run_bass_kernel_spmd

    nc = bacc.Bacc("TRN2", target_bir_lowering=False, num_devices=1)
    x = np.asarray(inputs["L0_attn_x"])
    arrays = {"x_dram": np.ascontiguousarray(x.reshape(-1, D))}
    for name, given in _W.items():
        arrays[f"w_{name}_dram"] = np.ascontiguousarray(np.asarray(inputs[given]).T)
    for name in ("mu_r", "mu_k"):
        arrays[f"{name}_dram"] = np.ascontiguousarray(np.asarray(inputs[f"L0_ffn_{name}"]).reshape(HALVES, P).T)

    def dram(name):
        return nc.dram_tensor(name, arrays[name].shape, F32, kind="ExternalInput").ap()

    out = nc.dram_tensor("out_dram", arrays["x_dram"].shape, F32, kind="ExternalOutput").ap()
    macaron(nc, dram("x_dram"), {name: dram(f"w_{name}_dram") for name in _W},
            dram("mu_r_dram"), dram("mu_k_dram"), out)
    r = run_bass_kernel_spmd(nc, [arrays], core_ids=[0])
    return r.results[0]["out_dram"].reshape(x.shape)
```
